# Optimizing a Trainium2 kernel written in Bass

```python
import numpy as np
import jax
import jax.numpy as jnp

def _softmax(x, axis=-1):
    return jax.nn.softmax(x, axis=axis)

def _gelu(x):
    return jax.nn.gelu(x, approximate=True)

def _silu(x):
    return jax.nn.silu(x)

def _sigmoid(x):
    return jax.nn.sigmoid(x)

def _layernorm(x, axis=-1, eps=1e-05):
    m = jnp.mean(x, axis=axis, keepdims=True)
    v = jnp.var(x, axis=axis, keepdims=True)
    return (x - m) / jnp.sqrt(v + eps)

def _scatter_add(tgt, idx, src, axis=0):
    return tgt.at[idx].add(src)

def _segment_sum(src, seg, n):
    return jax.ops.segment_sum(src, seg, n)
kernel_name = 'mk_cond_seq_d1_seqx_r4_f95b9b'

def setup_inputs(seed: int=0):
    np.random.seed(seed)
    _w = jnp.asarray

    def _rec_inputs():
        import jax
        import jax.numpy as jnp
        _rk = jax.random.key(seed)
        x = -0.0002928 + 1 * jax.random.normal(jax.random.fold_in(_rk, 1), (64, 64, 256), jnp.float32)
        _lenS = 64 - jax.random.randint(jax.random.fold_in(_rk, 7), (64,), 0, max(1, 64 // 4) + 1, jnp.int32)
        _lenS2 = 64 - jax.random.randint(jax.random.fold_in(_rk, 8), (64,), 0, max(1, 64 // 4) + 1, jnp.int32)
        cond_1024 = 0.0061147 + 1.02565 * jax.random.normal(jax.random.fold_in(_rk, 11), (64, 256), jnp.float32)
        return (x, cond_1024)
    x, cond_1024 = _rec_inputs()

    def _L0_cond_setup():
        import jax, jax.numpy as jnp
        import numpy as np
        B, T, DIM = (4, 256, 256)
        COND = 256
        HEADS, DH = (16, 64)
        INNER = HEADS * DH
        MLP = 1024
        EPS = 1e-05

        def _layernorm(x):
            mu = jnp.mean(x, axis=-1, keepdims=True)
            var = jnp.mean(jnp.square(x - mu), axis=-1, keepdims=True)
            return (x - mu) * jax.lax.rsqrt(var + EPS)

        def _modulate(x, shift, scale):
            return x * (1.0 + scale) + shift

        def _attention(x, W_qkv, W_out, b_out):
            Bq, Tq, _ = x.shape
            qkv = x @ W_qkv
            q, k, v = jnp.split(qkv, 3, axis=-1)
            q = q.reshape(Bq, Tq, HEADS, DH)
            k = k.reshape(Bq, Tq, HEADS, DH)
            v = v.reshape(Bq, Tq, HEADS, DH)
            scale = DH ** (-0.5)
            attn = jnp.einsum('bqhd,bkhd->bhqk', q, k) * scale
            attn = jax.nn.softmax(attn, axis=-1)
            out = jnp.einsum('bhqk,bkhd->bqhd', attn, v).reshape(Bq, Tq, INNER)
            return out @ W_out + b_out

        def _ff(x, W1, b1, W2, b2):
            return jax.nn.gelu(x @ W1 + b1, approximate=False) @ W2 + b2
        key = jax.random.key(seed)
        ks = jax.random.split(key, 12)
        s = 0.02
        return {'x': jax.random.normal(ks[0], (B, T, DIM), jnp.float32), 'c': jax.random.normal(ks[1], (B, 1, COND), jnp.float32), 'W_mod': jax.random.normal(ks[2], (COND, 6 * DIM), jnp.float32) * s, 'b_mod': jax.random.normal(ks[3], (6 * DIM,), jnp.float32) * s, 'W_qkv': jax.random.normal(ks[4], (DIM, 3 * INNER), jnp.float32) * s, 'W_out': jax.random.normal(ks[5], (INNER, DIM), jnp.float32) * s, 'b_out': jax.random.normal(ks[6], (DIM,), jnp.float32) * s, 'W1': jax.random.normal(ks[7], (DIM, MLP), jnp.float32) * s, 'b1': jax.random.normal(ks[8], (MLP,), jnp.float32) * s, 'W2': jax.random.normal(ks[9], (MLP, DIM), jnp.float32) * s, 'b2': jax.random.normal(ks[10], (DIM,), jnp.float32) * s}
    _L0_cond_all = _L0_cond_setup()
    _L0_cond_in = {k: v for k, v in _L0_cond_all.items() if k in ('W_mod', 'b_mod', 'W_qkv', 'W_out', 'b_out', 'W1', 'b1', 'W2', 'b2')}
    del _L0_cond_all
    return {'x': x, 'cond_1024': cond_1024, 'L0_cond_W_mod': _L0_cond_in['W_mod'], 'L0_cond_b_mod': _L0_cond_in['b_mod'], 'L0_cond_W_qkv': _L0_cond_in['W_qkv'], 'L0_cond_W_out': _L0_cond_in['W_out'], 'L0_cond_b_out': _L0_cond_in['b_out'], 'L0_cond_W1': _L0_cond_in['W1'], 'L0_cond_b1': _L0_cond_in['b1'], 'L0_cond_W2': _L0_cond_in['W2'], 'L0_cond_b2': _L0_cond_in['b2']}

def reference(x, cond_1024, L0_cond_W_mod, L0_cond_b_mod, L0_cond_W_qkv, L0_cond_W_out, L0_cond_b_out, L0_cond_W1, L0_cond_b1, L0_cond_W2, L0_cond_b2):
    import jax
    import jax.numpy as jnp

    def _L0_cond_ref(x, c, W_mod, b_mod, W_qkv, W_out, b_out, W1, b1, W2, b2):
        import jax, jax.numpy as jnp
        import numpy as np
        B, T, DIM = (4, 256, 256)
        COND = 256
        HEADS, DH = (16, 64)
        INNER = HEADS * DH
        MLP = 1024
        EPS = 1e-05

        def _layernorm(x):
            mu = jnp.mean(x, axis=-1, keepdims=True)
            var = jnp.mean(jnp.square(x - mu), axis=-1, keepdims=True)
            return (x - mu) * jax.lax.rsqrt(var + EPS)

        def _modulate(x, shift, scale):
            return x * (1.0 + scale) + shift

        def _attention(x, W_qkv, W_out, b_out):
            Bq, Tq, _ = x.shape
            qkv = x @ W_qkv
            q, k, v = jnp.split(qkv, 3, axis=-1)
            q = q.reshape(Bq, Tq, HEADS, DH)
            k = k.reshape(Bq, Tq, HEADS, DH)
            v = v.reshape(Bq, Tq, HEADS, DH)
            scale = DH ** (-0.5)
            attn = jnp.einsum('bqhd,bkhd->bhqk', q, k) * scale
            attn = jax.nn.softmax(attn, axis=-1)
            out = jnp.einsum('bhqk,bkhd->bqhd', attn, v).reshape(Bq, Tq, INNER)
            return out @ W_out + b_out

        def _ff(x, W1, b1, W2, b2):
            return jax.nn.gelu(x @ W1 + b1, approximate=False) @ W2 + b2
        mod = jax.nn.silu(c) @ W_mod + b_mod
        sh_msa, sc_msa, g_msa, sh_mlp, sc_mlp, g_mlp = jnp.split(mod, 6, axis=-1)
        x = x + g_msa * _attention(_modulate(_layernorm(x), sh_msa, sc_msa), W_qkv, W_out, b_out)
        x = x + g_mlp * _ff(_modulate(_layernorm(x), sh_mlp, sc_mlp), W1, b1, W2, b2)
        return x
    x = _L0_cond_ref(x, cond_1024[:, None, :], L0_cond_W_mod, L0_cond_b_mod, L0_cond_W_qkv, L0_cond_W_out, L0_cond_b_out, L0_cond_W1, L0_cond_b1, L0_cond_W2, L0_cond_b2)
    return x

_drawn_inputs = setup_inputs


def setup_inputs(seed=0):
    import zlib

    import numpy as np

    out = dict(_drawn_inputs(seed))
    spreads = {}
    factors = {'L0_cond_b_mod': 8.0,
     'L0_cond_W_qkv': 5.803,
     'L0_cond_W_out': 5.773,
     'L0_cond_b_out': 8.0,
     'L0_cond_b1': 51.127,
     'L0_cond_b2': 8.0,
     'L0_cond_W1': 3.091,
     'L0_cond_W2': 2.764}
    for name, (base, spread) in spreads.items():
        noise = np.random.default_rng([zlib.crc32(name.encode()), seed]).standard_normal(out[name].shape)
        drawn = base * np.exp(spread * noise) if base else spread * noise
        out[name] = jnp.asarray(drawn.astype(out[name].dtype))
    for name, factor in factors.items():
        out[name] = (out[name] * factor).astype(out[name].dtype)
    return out
```

```python
import concourse.bass as bass
from concourse import mybir
from contextlib import ExitStack

F32 = mybir.dt.float32
F32R = mybir.dt.float32r
ALU = mybir.AluOpType
ACT = mybir.ActivationFunctionType
AX = mybir.AxisListType

P = 128
BATCH, SEQ, DIM = 64, 64, 256
HEADS, DH = 16, 64
INNER = HEADS * DH
MLP = 1024
EPS = 1e-5
TILES = 2
TOK = TILES * P
NB = TOK // SEQ
STEPS = BATCH * SEQ // TOK
DC = DIM // P
PAIRS = HEADS // 2
MC = MLP // P
HALF = 512
HP = HALF // P
SH1, SC1, SH2, SC2 = range(4)


class Turn:

    def __init__(self, made, before):
        self.made, self.before = made, before


def turns(engine, s):
    if isinstance(s, int):
        counts = [s - 1, s, s + 1, s + 2]
    else:
        counts = [engine.snap(s - 1), s, engine.snap(s + 1), engine.snap(s + 2)]
    return [Turn(counts[i + 1], counts[i]) for i in range(3)]


def hold(engine, sem, count):
    if not isinstance(count, int) or count > 0:
        engine.wait_ge(sem, count)


def apart(engine, passed, count):
    if not isinstance(count, int):
        engine.sem_inc(passed, 1)


def dit_block_kernel(nc, x, cond, w_mod, b_mod, w_qkv, w_out, b_out, w1, b1, w2, b2, out):
    ctx = ExitStack()
    with ctx:
        def sb(name, shape, dt=F32):
            return ctx.enter_context(nc.sbuf_tensor(name, shape, dt))

        def sem(name):
            return ctx.enter_context(nc.semaphore(name))

        def sems(name, n):
            return [sem(f"{name}{i}") for i in range(n)]

        wqkv_hi, wqkv_lo = (sb(f"wqkv_{k}", [P, DC, 3 * INNER], F32R) for k in ("hi", "lo"))
        wout_hi, wout_lo = (sb(f"wout_{k}", [P, PAIRS, DIM], F32R) for k in ("hi", "lo"))
        w1_hi, w1_lo = (sb(f"w1_{k}", [P, DC, MLP], F32R) for k in ("hi", "lo"))
        w2_hi, w2_lo = (sb(f"w2_{k}", [P, MC, DIM], F32R) for k in ("hi", "lo"))
        qk = sb("qk", [P, 2 * PAIRS, TOK])
        v = sb("v", [P, TILES, INNER])
        probs = sb("probs", [P, TILES, 2, HALF])
        pt_gelu = sb("pt_gelu", [P, 4, HALF])
        probs_t, gelu = pt_gelu[:, 0:2, :], pt_gelu[:, 2:4, :]
        att_hi, att_lo = (sb(f"att_{k}", [P, TILES, PAIRS, P], F32R) for k in ("hi", "lo"))
        g_hi, g_lo = (sb(f"g_{k}", [P, MC, TOK], F32R) for k in ("hi", "lo"))
        h1_hi, h1_lo = (sb(f"h1_{k}", [P, DC, TOK], F32R) for k in ("hi", "lo"))
        h2_hi, h2_lo = (sb(f"h2_{k}", [P, DC, TOK], F32R) for k in ("hi", "lo"))
        h1 = sb("h1", [P, DC, TOK])
        h2 = sb("h2", [P, DC, TOK])
        x_ln, xn1, x_res, xn2, gate1, gate2, o_buf, x2, y_buf = (
            sb(n, [P, TILES, DIM]) for n in
            ("x_ln", "xn1", "x_res", "xn2", "gate1", "gate2", "o_buf", "x2", "y_buf"))
        bout_bc = sb("bout_bc", [P, DIM])
        b2_bc = sb("b2_bc", [P, DIM])
        b1_col = sb("b1_col", [P, MC])
        mod_t = sb("mod_t", [P, 4, DC, BATCH])
        ident = sb("ident", [P, P])
        ones = sb("ones", [1, BATCH])
        minus_half = sb("minus_half", [P, TILES])
        eps = sb("eps", [P, TILES])
        stats1 = sb("stats1", [P, TILES, 6])
        stats2 = sb("stats2", [P, TILES, 6])
        mv1 = sb("mv1", [P, TILES, 2])
        mv2 = sb("mv2", [P, TILES, 2])
        rstd1 = sb("rstd1", [P, TILES])
        rstd2 = sb("rstd2", [P, TILES])
        var1 = sb("var1", [P, TILES])
        var2 = sb("var2", [P, TILES])
        row_max = sb("row_max", [P, TILES, 2, 2 * HP])
        row_sum = sb("row_sum", [P, TILES, 2, 2 * HP])
        row_inv = sb("row_inv", [P, TILES, 2, 2 * HP])
        wmod = qk[:, :, :].rearrange("p a b -> p (a b)")[:, 0:DC * 6 * DIM].rearrange("p (c n) -> p c n", c=DC)
        c_in, c_exp = x2[0:BATCH, 0, :], x2[0:BATCH, 1, :]
        silu = o_buf[0:BATCH, 0, :]
        silu_t = o_buf[:, 1, 0:DC * BATCH].rearrange("p (c b) -> p c b", c=DC)
        gates = y_buf[0:BATCH, :, :]
        bmod_row = pt_gelu[0:1, :, :].rearrange("p a b -> p (a b)")[:, 0:6 * DIM]
        stage = [v[:, :, :].rearrange("p t n -> p (t n)"),
                 probs[:, :, :, :].rearrange("p t a n -> p (t a n)"),
                 pt_gelu[:, :, :].rearrange("p a n -> p (a n)")]
        gate_rows = nc.dram_tensor("gate_rows", (BATCH, 2, DIM), F32, kind="Internal").ap()

        dense = [ctx.enter_context(nc.psum_tensor(f"dense{i}", [P, 2, TOK], F32)) for i in range(3)]
        s_ps = [ctx.enter_context(nc.psum_tensor(f"scores{i}", [P, HALF], F32)) for i in range(2)]
        pt_ps = ctx.enter_context(nc.psum_tensor("probs_t_ps", [P, HALF], F32))
        av_ps = [ctx.enter_context(nc.psum_tensor(f"att{i}", [P, HALF], F32)) for i in range(2)]

        cond_in, wmod_in, consts_in = sem("cond_in"), sem("wmod_in"), sem("consts_in")
        stage_in, w_hi_made, w_lo_made = sems("stage_in", 3), sem("w_hi_made"), sem("w_lo_made")
        filled, ident_made, ones_made = sem("filled"), sem("ident_made"), sem("ones_made")
        c_exp_made, silu_step, silu_t_ps = sem("c_exp_made"), sem("silu_step"), sem("silu_t_ps")
        silu_t_made, mod_ps, mod_made, gates_made = sem("silu_t_made"), sem("mod_ps"), sem("mod_made"), sem("gates_made")
        x_in, xres_in, gate1_in, gate2_in, stored = (sem(n) for n in ("x_in", "xres_in", "gate1_in", "gate2_in", "stored"))
        s_done, v_done, pt_done, av_done = sems("s_done", 4), sems("v_done", 4), sems("pt_done", 4), sems("av_done", 4)
        ln1t_done, ln2t_done = sem("ln1t_done"), sem("ln2t_done")
        qk_done, ff1_done, ff2_done, o_done = sems("qk_done", 8), sems("ff1_done", 4), sems("ff2_done", 2), sems("o_done", 2)
        pe_passed, dve_passed = sem("pe_passed"), sem("dve_passed")
        exp_made, v_made, pt_made, att_hi_made = sems("exp_made", 4), sems("v_made", 4), sems("pt_made", 4), sems("att_hi_made", 4)
        qk_made, gelu_made = sems("qk_made", 8), sems("gelu_made", 4)
        h1_hi_made, h2_hi_made = sem("h1_hi_made"), sem("h2_hi_made")
        max_made, sub_made, sum_made, inv_made = sems("max_made", 2), sems("sub_made", 4), sems("sum_made", 2), sems("inv_made", 2)
        scaled1, scaled2, h1_lo_made, h2_lo_made = sem("scaled1"), sem("scaled2"), sem("h1_lo_made"), sem("h2_lo_made")
        stats1_made, stats2_made = sems("stats1_made", 2), sems("stats2_made", 2)
        mv1_made, mv2_made, xn1_made, xn2_made = sem("mv1_made"), sems("mv2_made", 2), sems("xn1_made", 2), sems("xn2_made", 2)
        g_hi_made, g_lo_made, att_lo_made = sems("g_hi_made", 4), sems("g_lo_made", 4), sems("att_lo_made", 4)
        o_biased, y_biased = sems("o_biased", 2), sems("y_biased", 2)
        var1_made, rstd1_made, var2_made, rstd2_made = sem("var1_made"), sem("rstd1_made"), sems("var2_made", 2), sems("rstd2_made", 2)
        norm_made, h1_made, h2_made = sems("norm_made", 4), sem("h1_made"), sem("h2_made")
        o_gated, x2_made, y_gated, y_made = sems("o_gated", 2), sems("x2_made", 2), sems("y_gated", 2), sems("y_made", 2)

        x_v = x.rearrange("b q d -> (b q) d").rearrange("(s t p) d -> s p t d", t=TILES, p=P)
        out_v = out.rearrange("b q d -> (b q) d").rearrange("(s t p) d -> s p t d", t=TILES, p=P)
        gates_v = gate_rows.rearrange("(s t b) g d -> s b g t d", t=TILES, b=2)


        block = ctx.enter_context(nc.Block())

        @block.sync
        def _(sp):
            sp.dma_start(c_in, cond).then_inc(cond_in, 16)
            sp.dma_start(bmod_row, b_mod.rearrange("(o n) -> o n", o=1)).then_inc(wmod_in, 16)
            sp.dma_start(wmod, w_mod.rearrange("(c p) n -> p c n", p=P)).then_inc(wmod_in, 16)

            def load_x(d, turn):
                hold(sp, xn1_made[1], turn.before)
                src = x_v[d] if isinstance(d, int) else x_v[bass.ds(d, 1), :, :, :].squeeze(0)
                sp.dma_start(x_ln[:, :, :], src).then_inc(x_in, 16)

            def load_res(d, turn):
                hold(sp, x2_made[1], turn.before)
                src = x_v[d] if isinstance(d, int) else x_v[bass.ds(d, 1), :, :, :].squeeze(0)
                sp.dma_start(x_res[:, :, :], src).then_inc(xres_in, 16)
                load_gate(gate1, 0, d, gate1_in)

            def load_gate(tile, g, d, loaded):
                for b in range(2):
                    src = gates_v[d, b, g] if isinstance(d, int) else gates_v[bass.ds(d, 1), b, g, :, :].squeeze(0)
                    sp.dma_start(tile[SEQ * b:SEQ * (b + 1), :, :], src.partition_broadcast(SEQ)).then_inc(loaded, 16)

            def finish(d, turn):
                sp.wait_ge(y_made[0], turn.made)
                sp.wait_ge(y_made[1], turn.made)
                dst = out_v[d] if isinstance(d, int) else out_v[bass.ds(d, 1), :, :, :].squeeze(0)
                sp.dma_start(dst, y_buf[:, :, :]).then_inc(stored, 16)

            load_x(0, Turn(1, 0))
            wq_v = w_qkv.rearrange("(c p) n -> p c n", p=P)
            sources = [wq_v[:, :, 0:INNER], wq_v[:, :, INNER:2 * INNER], wq_v[:, :, 2 * INNER:3 * INNER],
                       w_out.rearrange("(c p) n -> p c n", p=P), w1.rearrange("(c p) n -> p c n", p=P),
                       w2.rearrange("(c p) n -> p c n", p=P)]
            for i, src in enumerate(sources):
                if i == 2:
                    sp.wait_ge(mod_ps, 2)
                if i >= 3:
                    sp.wait_ge(w_hi_made, i - 2)
                    sp.wait_ge(w_lo_made, i - 2)
                sp.dma_start(stage[i % 3].rearrange("p (c n) -> p c n", c=src.shape[1]), src).then_inc(stage_in[i % 3], 16)
                if i == 1:
                    sp.dma_start(bout_bc[:, :], b_out.partition_broadcast(P)).then_inc(consts_in, 16)
                    sp.dma_start(b2_bc[:, :], b2.partition_broadcast(P)).then_inc(consts_in, 16)
                    sp.dma_start(b1_col[:, :], b1.rearrange("(m p) -> p m", p=P),
                                 allow_slow_non_contiguous=True).then_inc(consts_in, 16)
                    sp.wait_ge(gates_made, 1)
                    sp.dma_start(gate_rows, gates).then_inc(stored, 16)
                if i == 2:
                    load_x(1, Turn(2, 1))
            sp.wait_ge(stored, 16)
            load_res(0, Turn(1, 0))
            load_gate(gate2, 1, 0, gate2_in)

            def step(s, has_next=True):
                prev, this, nxt = turns(sp, s)
                if has_next:
                    load_x(s + 1 if isinstance(s, int) else sp.snap(s + 1), nxt)
                load_res(s, this)
                finish(s - 1 if isinstance(s, int) else sp.snap(s - 1), prev)
                load_gate(gate2, 1, s, gate2_in)

            with sp.Fori(1, STEPS - 1) as s:
                step(s)
            step(STEPS - 1, has_next=False)
            finish(STEPS - 1, Turn(STEPS, STEPS - 1))
            sp.wait_ge(stored, 16 * (STEPS + 1))

        @block.tensor
        def _(pe):
            drained = {}

            def three_products(ps, terms, done=None):
                n = len(terms)
                for i, (a_hi, a_lo, b_hi, b_lo) in enumerate(terms):
                    pe_mm(ps, a_hi, b_hi, i == 0, False)
                    pe_mm(ps, a_hi, b_lo, False, False)
                    last = pe_mm(ps, a_lo, b_hi, False, i == n - 1)
                if done is not None:
                    last.then_inc(done, 1)

            def pe_mm(ps, a, b, start, stop):
                return nc.tensor.matmul(ps, a, b, start=start, stop=stop)

            def scores(t, this):
                for half in range(2):
                    hold(pe, sub_made[2 * (1 - t) + half], this.before if t == 0 else this.made)
                    if half == 0 and t == 0:
                        for u in range(8):
                            pe.wait_ge(qk_made[u], this.made)
                    apart(pe, pe_passed, this.made)
                    for i in range(HP):
                        pair = HP * half + i
                        for b in range(2):
                            tok = slice(t * P + b * SEQ, t * P + (b + 1) * SEQ)
                            for h in range(2):
                                rows = slice(DH * h, DH * (h + 1))
                                last = pe_mm(s_ps[half][rows, i * P + b * SEQ:i * P + (b + 1) * SEQ],
                                             qk[rows, pair, tok], qk[rows, PAIRS + pair, tok], True, True)
                    last.then_inc(s_done[2 * t + half], 1)

            def values(u, this):
                t, n = divmod(u, 2)
                bank = u % 3
                hold(pe, *drained[bank])
                if u == 0:
                    pe.wait_ge(h1_hi_made, this.made)
                    pe.wait_ge(h1_lo_made, this.made)
                tok, cols = slice(t * P, (t + 1) * P), slice(2 * INNER + n * HALF, 2 * INNER + (n + 1) * HALF)
                three_products(dense[bank][:, :, :].rearrange("p a b -> p (a b)"),
                               [(h1_hi[:, c, tok], h1_lo[:, c, tok], wqkv_hi[:, c, cols], wqkv_lo[:, c, cols])
                                for c in range(DC)], v_done[u])
                drained[bank] = (v_made[u], this.made)

            def transposed(xn, bank, made, done, drain, turn):
                hold(pe, *drained[bank])
                pe.wait_ge(made[0], turn.made)
                pe.wait_ge(made[1], turn.made)
                for t in range(TILES):
                    for c in range(DC):
                        last = nc.tensor.transpose(dense[bank][:, c, t * P:(t + 1) * P], xn[:, t, c * P:(c + 1) * P], ident[:, :])
                last.then_inc(done, 1)
                drained[bank] = (drain, turn.made)

            def ff1(u, prev):
                bank = u % 3
                hold(pe, *drained[bank])
                if u == 0:
                    pe.wait_ge(h2_hi_made, prev.made)
                    pe.wait_ge(h2_lo_made, prev.made)
                for j in range(2):
                    cols = slice((2 * u + j) * P, (2 * u + j + 1) * P)
                    three_products(dense[bank][:, j, :],
                                   [(w1_hi[:, c, cols], w1_lo[:, c, cols], h2_hi[:, c, :], h2_lo[:, c, :])
                                    for c in range(DC)], ff1_done[u] if j == 1 else None)
                drained[bank] = (gelu_made[u], prev.made)

            def project_qk(u, nxt):
                bank = (u + 1) % 3 if u < 6 else u - 5
                hold(pe, *drained[bank])
                if u == 0:
                    pe.wait_ge(h1_hi_made, nxt.made)
                    pe.wait_ge(h1_lo_made, nxt.made)
                for j in range(2):
                    cols = slice((2 * u + j) * P, (2 * u + j + 1) * P)
                    three_products(dense[bank][:, j, :],
                                   [(wqkv_hi[:, c, cols], wqkv_lo[:, c, cols], h1_hi[:, c, :], h1_lo[:, c, :])
                                    for c in range(DC)], qk_done[u] if j == 1 else None)
                drained[bank] = (qk_made[u], nxt.made)

            def transpose_probs(t, half, this):
                n = 2 * t + half
                hold(pe, pt_made[(n - 1) % 4], this.before if n == 0 else this.made)
                pe.wait_ge(norm_made[n], this.made)
                for i in range(HP):
                    last = nc.tensor.transpose(pt_ps[:, i * P:(i + 1) * P], probs[:, t, half, i * P:(i + 1) * P], ident[:, :])
                last.then_inc(pt_done[n], 1)

            def attend(t, this):
                if t == 0:
                    for u in range(4):
                        pe.wait_ge(v_made[u], this.made)
                for half in range(2):
                    for b in range(2):
                        if half == 0:
                            hold(pe, att_lo_made[2 * (1 - t) + b], this.before if t == 0 else this.made)
                    pe.wait_ge(pt_made[2 * t + half], this.made)
                    apart(pe, pe_passed, this.made)
                    for pair in range(HP * half, HP * (half + 1)):
                        for b in range(2):
                            keys = slice(SEQ * b, SEQ * (b + 1))
                            for h in range(2):
                                head, col = 2 * pair + h, (pair % HP) * P + h * SEQ
                                last = pe_mm(av_ps[b][DH * h:DH * (h + 1), pair * SEQ:(pair + 1) * SEQ],
                                             v[keys, t, head * DH:(head + 1) * DH], probs_t[keys, half, col:col + SEQ], True, True)
                            if half == 1 and pair == PAIRS - 1:
                                last.then_inc(av_done[2 * t + b], 1)

            def project_out(t, this):
                bank = 0
                hold(pe, *drained[bank])
                for b in range(2):
                    pe.wait_ge(att_hi_made[2 * t + b], this.made)
                    pe.wait_ge(att_lo_made[2 * t + b], this.made)
                three_products(dense[bank][:, 0, :],
                               [(att_hi[:, t, c, :], att_lo[:, t, c, :], wout_hi[:, c, :], wout_lo[:, c, :])
                                for c in range(PAIRS)], o_done[t])
                drained[bank] = (o_biased[t], this.made)

            def ff2(t, prev):
                bank = 1 + t
                hold(pe, *drained[bank])
                if t == 0:
                    for u in range(4):
                        pe.wait_ge(g_hi_made[u], prev.made)
                        pe.wait_ge(g_lo_made[u], prev.made)
                tok = slice(t * P, (t + 1) * P)
                three_products(dense[bank][:, 0, :],
                               [(g_hi[:, m, tok], g_lo[:, m, tok], w2_hi[:, m, :], w2_lo[:, m, :])
                                for m in range(MC)], ff2_done[t])
                drained[bank] = (y_biased[t], prev.made)

            def step(s, has_prev=True, has_next=True):
                prev, this, nxt = turns(pe, s)
                if has_prev:
                    drained[0] = (o_biased[1], prev.made)
                    drained[1], drained[2] = (qk_made[6], this.made), (qk_made[7], this.made)
                scores(0, this)
                if not has_prev:
                    pe.wait_ge(w_hi_made, 6)
                    pe.wait_ge(w_lo_made, 6)
                for u in range(4):
                    values(u, this)
                if has_prev:
                    transposed(xn2, 1, xn2_made, ln2t_done, scaled2, prev)
                scores(1, this)
                if has_next:
                    transposed(xn1, 2, xn1_made, ln1t_done, scaled1, nxt)
                if has_prev:
                    for u in range(4):
                        ff1(u, prev)
                transpose_probs(0, 0, this)
                transpose_probs(0, 1, this)
                if has_next:
                    project_qk(0, nxt)
                    project_qk(1, nxt)
                attend(0, this)
                if has_next:
                    project_qk(2, nxt)
                    project_qk(3, nxt)
                transpose_probs(1, 0, this)
                if has_next:
                    project_qk(4, nxt)
                transpose_probs(1, 1, this)
                if has_next:
                    project_qk(5, nxt)
                if has_prev:
                    ff2(0, prev)
                    ff2(1, prev)
                project_out(0, this)
                attend(1, this)
                if has_next:
                    project_qk(6, nxt)
                    project_qk(7, nxt)
                project_out(1, this)

            pe.wait_ge(ident_made, 1)
            pe.wait_ge(ones_made, 1)
            pe.wait_ge(silu_step, 3)
            for c in range(DC):
                last = nc.tensor.transpose(s_ps[0][:, c * BATCH:(c + 1) * BATCH], silu[:, c * P:(c + 1) * P], ident[0:BATCH, 0:BATCH])
            last.then_inc(silu_t_ps, 1)
            pe.wait_ge(silu_t_made, 1)
            pe.wait_ge(wmod_in, 32)
            for k, section in enumerate((0, 1, 3, 4)):
                for c in range(DC):
                    cols = slice(section * DIM + c * P, section * DIM + (c + 1) * P)
                    ps = av_ps[0][:, (k * DC + c) * BATCH:(k * DC + c + 1) * BATCH]
                    for kc in range(DC):
                        pe_mm(ps, wmod[:, kc, cols], silu_t[:, kc, :], kc == 0, False)
                    last = pe_mm(ps, bmod_row[:, cols], ones[:, :], False, True)
            last.then_inc(mod_ps, 1)
            for g, section in enumerate((2, 5)):
                cols = slice(section * DIM, (section + 1) * DIM)
                ps = av_ps[1][0:BATCH, g * DIM:(g + 1) * DIM]
                for kc in range(DC):
                    pe_mm(ps, silu_t[:, kc, :], wmod[:, kc, cols], kc == 0, False)
                last = pe_mm(ps, ones[:, :], bmod_row[:, cols], False, True)
            last.then_inc(mod_ps, 1)

            first = Turn(1, 0)
            drained.update({b: (mod_ps, 0) for b in range(3)})
            transposed(xn1, 2, xn1_made, ln1t_done, scaled1, first)
            pe.wait_ge(w_hi_made, 2)
            pe.wait_ge(w_lo_made, 2)
            for u in range(8):
                project_qk(u, first)
            step(0, has_prev=False)
            with pe.Fori(1, STEPS - 1) as s:
                step(s)
            step(STEPS - 1, has_next=False)
            last = Turn(STEPS, STEPS - 1)
            transposed(xn2, 1, xn2_made, ln2t_done, scaled2, last)
            for u in range(4):
                ff1(u, last)
            ff2(0, last)
            ff2(1, last)

        @block.scalar
        def _(act):
            def copy_bank(dst, src, made):
                nc.scalar.activation(dst, src, ACT.Copy).then_inc(made, 1)

            def high_part(dst, src, whole_made, made, turn):
                act.wait_ge(whole_made, turn.made)
                nc.scalar.activation(dst[:, :, :], src[:, :, :], ACT.Copy).then_inc(made, 1)

            def flat(ps):
                return ps[:, :, :].rearrange("p a b -> p (a b)")

            def exps(t, this):
                for half in range(2):
                    n = 2 * t + half
                    act.wait_ge(sub_made[n], this.made)
                    e = probs[:, t, half, :]
                    nc.scalar.activation(e, e, ACT.Exp, scale=DH ** -0.5).then_inc(exp_made[n], 1)

            def take_v(u, this):
                act.wait_ge(v_done[u], this.made)
                t, n = divmod(u, 2)
                copy_bank(v[:, t, n * HALF:(n + 1) * HALF], flat(dense[u % 3]), v_made[u])

            def take_qk(u, nxt):
                act.wait_ge(qk_done[u], nxt.made)
                bank = (u + 1) % 3 if u < 6 else u - 5
                copy_bank(qk[:, 2 * u:2 * u + 2, :], dense[bank][:, :, :], qk_made[u])

            def gelus(u, prev):
                act.wait_ge(ff1_done[u], prev.made)
                if u >= 2:
                    act.wait_ge(g_lo_made[u - 2], prev.made)
                for j in range(2):
                    m = 2 * u + j
                    last = nc.scalar.activation(gelu[:, u % 2, j * TOK:(j + 1) * TOK], dense[u % 3][:, j, :], ACT.Gelu,
                                                bias=b1_col[:, m:m + 1])
                last.then_inc(gelu_made[u], 1)

            def take_pt(t, half, this):
                n = 2 * t + half
                act.wait_ge(pt_done[n], this.made)
                copy_bank(probs_t[:, half, :], pt_ps[:, :], pt_made[n])

            def att_high(t, this):
                for b in range(2):
                    n = 2 * t + b
                    act.wait_ge(av_done[n], this.made)
                    copy_bank(att_hi[:, t, :, SEQ * b:SEQ * (b + 1)], av_ps[b][:, :].rearrange("p (i q) -> p i q", i=PAIRS),
                              att_hi_made[n])

            def step(s, has_prev=True, has_next=True):
                prev, this, nxt = turns(act, s)
                if not has_prev:
                    act.wait_ge(w_lo_made, 6)
                take_v(0, this)
                exps(0, this)
                for u in range(1, 4):
                    take_v(u, this)
                if has_prev:
                    high_part(h2_hi, h2, h2_made, h2_hi_made, prev)
                exps(1, this)
                if has_next:
                    high_part(h1_hi, h1, h1_made, h1_hi_made, nxt)
                if has_prev:
                    for u in range(4):
                        gelus(u, prev)
                take_pt(0, 0, this)
                take_pt(0, 1, this)
                if has_next:
                    take_qk(0, nxt)
                    take_qk(1, nxt)
                att_high(0, this)
                if has_next:
                    take_qk(2, nxt)
                    take_qk(3, nxt)
                take_pt(1, 0, this)
                if has_next:
                    take_qk(4, nxt)
                take_pt(1, 1, this)
                if has_next:
                    take_qk(5, nxt)
                att_high(1, this)
                if has_next:
                    take_qk(6, nxt)
                    take_qk(7, nxt)

            act.wait_ge(cond_in, 16)
            nc.scalar.activation(c_exp, c_in, ACT.Exp, scale=-1.0).then_inc(c_exp_made, 1)
            act.wait_ge(silu_t_ps, 1)
            copy_bank(silu_t, s_ps[0][:, 0:DC * BATCH].rearrange("p (c b) -> p c b", c=DC), silu_t_made)
            act.wait_ge(mod_ps, 2)
            copy_bank(gates, av_ps[1][0:BATCH, :].rearrange("p (g d) -> p g d", g=2), gates_made)
            first = Turn(1, 0)
            targets = [wqkv_hi[:, :, 0:INNER], wqkv_hi[:, :, INNER:2 * INNER], wqkv_hi[:, :, 2 * INNER:], wout_hi, w1_hi, w2_hi]

            def split_weights(i):
                act.wait_ge(stage_in[i % 3], 16 * (i // 3 + 1))
                dst = targets[i][:, :, :]
                nc.scalar.activation(dst, stage[i % 3].rearrange("p (c n) -> p c n", c=dst.shape[1]), ACT.Copy).then_inc(w_hi_made, 1)

            split_weights(0)
            split_weights(1)
            high_part(h1_hi, h1, h1_made, h1_hi_made, first)
            for i in range(2, 6):
                split_weights(i)
                take_qk(2 * (i - 2), first)
                take_qk(2 * (i - 2) + 1, first)
            act.wait_ge(consts_in, 48)
            step(0, has_prev=False)
            with act.Fori(1, STEPS - 1) as s:
                step(s)
            step(STEPS - 1, has_next=False)
            last = Turn(STEPS, STEPS - 1)
            high_part(h2_hi, h2, h2_made, h2_hi_made, last)
            for u in range(4):
                gelus(u, last)

        @block.vector
        def _(dve):
            def heads(ap):
                return ap.rearrange("p (g k) -> p g k", k=SEQ)

            def by_row(ap):
                return ap.unsqueeze(2).to_broadcast([P, 2 * HP, SEQ])

            def maxima(t, half, this):
                n = 2 * t + half
                dve.wait_ge(s_done[n], this.made)
                last = nc.vector.tensor_reduce(row_max[:, t, half, :], heads(s_ps[half][:, :]), AX.X, ALU.max)
                if half == 1:
                    last.then_inc(max_made[t], 1)

            def subtract(t, half, this):
                n = 2 * t + half
                if half == 0:
                    dve.wait_ge(max_made[t], this.made)
                nc.vector.tensor_tensor(heads(probs[:, t, half, :]), heads(s_ps[half][:, :]), by_row(row_max[:, t, half, :]),
                                        ALU.subtract).then_inc(sub_made[n], 1)

            def sums(t, this):
                for half in range(2):
                    n = 2 * t + half
                    dve.wait_ge(exp_made[n], this.made)
                    last = nc.vector.tensor_reduce(row_sum[:, t, half, :], heads(probs[:, t, half, :]), AX.X, ALU.add)
                last.then_inc(sum_made[t], 1)
                dve.wait_ge(sum_made[t], this.made)
                nc.vector.reciprocal(row_inv[:, t, :, :], row_sum[:, t, :, :]).then_inc(inv_made[t], 1)

            def row_stats(src, t, stats, mv, stats_made, mv_done, turn):
                nc.vector.bn_stats(stats[:, t, :], src[:, t, :]).then_inc(stats_made[t], 1)
                dve.wait_ge(stats_made[t], turn.made)
                apart(dve, dve_passed, turn.made)
                last = nc.vector.bn_aggr(mv[:, t, :], stats[:, t, :])
                if mv_done is not None:
                    last.then_inc(mv_done, 1)

            def normalise(src, t, mv, rstd, dst, made):
                nc.vector.tensor_scalar(dst[:, t, :], src[:, t, :], mv[:, t, 0:1], rstd[:, t:t + 1],
                                        ALU.subtract, ALU.mult).then_inc(made[t], 1)

            def ln1_stats(d, turn, loaded):
                dve.wait_ge(x_in, loaded)
                for t in range(TILES):
                    row_stats(x_ln, t, stats1, mv1, stats1_made, mv1_made if t == 1 else None, turn)

            def ln1_rows(turn):
                dve.wait_ge(rstd1_made, turn.made)
                for t in range(TILES):
                    normalise(x_ln, t, mv1, rstd1, xn1, xn1_made)

            def scale(bank, section, h, done, made, d, turn):
                dve.wait_ge(done, turn.made)
                at_b = slice(d * NB, (d + 1) * NB) if isinstance(d, int) else bass.ds(d * NB, NB)
                nc.vector.tensor_tensor(h[:, :, :].rearrange("p c (b k) -> p c b k", b=NB),
                                        dense[bank][:, :, :].rearrange("p c (b k) -> p c b k", b=NB),
                                        mod_t[:, section, :, at_b].unsqueeze(3).to_broadcast([P, DC, NB, SEQ]),
                                        ALU.mult).then_inc(made, 1)

            def low_part(lo, src, hi, hi_made, made, turn):
                dve.wait_ge(hi_made, turn.made)
                nc.vector.tensor_tensor(lo[:, :, :], src[:, :, :], hi[:, :, :].bitcast(F32), ALU.subtract).then_inc(made, 1)

            def split_gelu(u, prev):
                dve.wait_ge(gelu_made[u], prev.made)
                g = gelu[:, u % 2, :].rearrange("p (a b) -> p a b", a=2)
                hi, lo = g_hi[:, 2 * u:2 * u + 2, :], g_lo[:, 2 * u:2 * u + 2, :]
                nc.vector.tensor_copy(hi, g).then_inc(g_hi_made[u], 1)
                dve.wait_ge(g_hi_made[u], prev.made)
                nc.vector.tensor_tensor(lo, g, hi.bitcast(F32), ALU.subtract).then_inc(g_lo_made[u], 1)

            def att_low(t, this):
                for b in range(2):
                    n = 2 * t + b
                    dve.wait_ge(att_hi_made[n], this.made)
                    cols = slice(SEQ * b, SEQ * (b + 1))
                    nc.vector.tensor_tensor(att_lo[:, t, :, cols], av_ps[b][:, :].rearrange("p (i q) -> p i q", i=PAIRS),
                                            att_hi[:, t, :, cols].bitcast(F32), ALU.subtract).then_inc(att_lo_made[n], 1)

            def add_bias(t, bank, done, bias, dst, made, turn):
                dve.wait_ge(done[t], turn.made)
                nc.vector.tensor_tensor(dst[:, t, :], dense[bank][:, 0, :], bias[:, :], ALU.add).then_inc(made[t], 1)

            def ln2_stats(t, this):
                dve.wait_ge(x2_made[t], this.made)
                row_stats(x2, t, stats2, mv2, stats2_made, mv2_made[t], this)

            def ln2_rows(t, this):
                dve.wait_ge(rstd2_made[t], this.made)
                normalise(x2, t, mv2, rstd2, xn2, xn2_made)

            def step(s, has_prev=True, has_next=True):
                prev, this, nxt = turns(dve, s)
                fixed = isinstance(s, int)
                maxima(0, 0, this)
                maxima(0, 1, this)
                subtract(0, 0, this)
                subtract(0, 1, this)
                if has_next:
                    ln1_stats(None, nxt, 16 * (s + 2) if fixed else dve.snap(s * 16 + 32))
                sums(0, this)
                if has_next:
                    ln1_rows(nxt)
                if has_prev:
                    scale(1, SC2, h2, ln2t_done, scaled2, s - 1 if fixed else dve.snap(s - 1), prev)
                maxima(1, 0, this)
                if has_prev:
                    low_part(h2_lo, h2, h2_hi, h2_hi_made, h2_lo_made, prev)
                maxima(1, 1, this)
                subtract(1, 0, this)
                subtract(1, 1, this)
                if has_next:
                    scale(2, SC1, h1, ln1t_done, scaled1, s + 1 if fixed else dve.snap(s + 1), nxt)
                sums(1, this)
                if has_next:
                    low_part(h1_lo, h1, h1_hi, h1_hi_made, h1_lo_made, nxt)
                if has_prev:
                    for u in range(4):
                        split_gelu(u, prev)
                att_low(0, this)
                if has_prev:
                    dve.wait_ge(stored, 16 * s if fixed else dve.snap(s * 16))
                    add_bias(0, 1, ff2_done, b2_bc, y_buf, y_biased, prev)
                    add_bias(1, 2, ff2_done, b2_bc, y_buf, y_biased, prev)
                add_bias(0, 0, o_done, bout_bc, o_buf, o_biased, this)
                att_low(1, this)
                ln2_stats(0, this)
                ln2_rows(0, this)
                add_bias(1, 0, o_done, bout_bc, o_buf, o_biased, this)
                ln2_stats(1, this)
                ln2_rows(1, this)

            nc.vector.memset(ones[:, :], 1.0).then_inc(ones_made, 1)
            dve.wait_ge(c_exp_made, 1)
            nc.vector.tensor_scalar(c_exp, c_exp, 1.0, None, ALU.add).then_inc(silu_step, 1)
            dve.wait_ge(silu_step, 1)
            nc.vector.reciprocal(c_exp, c_exp).then_inc(silu_step, 1)
            dve.wait_ge(silu_step, 2)
            nc.vector.tensor_tensor(silu, c_in, c_exp, ALU.mult).then_inc(silu_step, 1)
            first, second = Turn(1, 0), Turn(2, 1)
            ln1_stats(0, first, 16)
            ln1_rows(first)
            dve.wait_ge(mod_ps, 1)
            for k in range(4):
                ps = av_ps[0][:, k * DC * BATCH:(k + 1) * DC * BATCH].rearrange("p (c b) -> p c b", c=DC)
                if k in (SC1, SC2):
                    nc.vector.tensor_scalar(mod_t[:, k, :, :], ps, 1.0, None, ALU.add).then_inc(mod_made, 1)
                else:
                    nc.vector.tensor_copy(mod_t[:, k, :, :], ps).then_inc(mod_made, 1)
            dve.wait_ge(mod_made, 4)
            targets = [(wqkv_hi[:, :, 0:INNER], wqkv_lo[:, :, 0:INNER]),
                       (wqkv_hi[:, :, INNER:2 * INNER], wqkv_lo[:, :, INNER:2 * INNER]),
                       (wqkv_hi[:, :, 2 * INNER:], wqkv_lo[:, :, 2 * INNER:]),
                       (wout_hi, wout_lo), (w1_hi, w1_lo), (w2_hi, w2_lo)]

            def split_weights(i):
                dve.wait_ge(w_hi_made, i + 1)
                hi, lo = (w[:, :, :] for w in targets[i])
                nc.vector.tensor_tensor(lo, stage[i % 3].rearrange("p (c n) -> p c n", c=hi.shape[1]), hi.bitcast(F32),
                                        ALU.subtract).then_inc(w_lo_made, 1)

            scale(2, SC1, h1, ln1t_done, scaled1, 0, first)
            split_weights(0)
            split_weights(1)
            low_part(h1_lo, h1, h1_hi, h1_hi_made, h1_lo_made, first)
            for i in range(2, 6):
                split_weights(i)
            dve.wait_ge(consts_in, 48)
            step(0, has_prev=False)
            with dve.Fori(1, STEPS - 1) as s:
                step(s)
            step(STEPS - 1, has_next=False)
            last = Turn(STEPS, STEPS - 1)
            scale(1, SC2, h2, ln2t_done, scaled2, STEPS - 1, last)
            low_part(h2_lo, h2, h2_hi, h2_hi_made, h2_lo_made, last)
            for u in range(4):
                split_gelu(u, last)
            dve.wait_ge(stored, 16 * STEPS)
            add_bias(0, 1, ff2_done, b2_bc, y_buf, y_biased, last)
            add_bias(1, 2, ff2_done, b2_bc, y_buf, y_biased, last)

        @block.gpsimd
        def _(pool):
            def reciprocal_root(mv, var, rstd, var_done, rstd_done, count, width):
                nc.gpsimd.tensor_tensor(var, mv, eps[:, 0:width], ALU.add).then_inc(var_done, 1)
                pool.wait_ge(var_done, count)
                nc.gpsimd.tensor_tensor(rstd, var, minus_half[:, 0:width], ALU.pow).then_inc(rstd_done, 1)

            def ln1_root(turn):
                pool.wait_ge(mv1_made, turn.made)
                reciprocal_root(mv1[:, :, 1], var1[:, :], rstd1[:, :], var1_made, rstd1_made, turn.made, TILES)

            def ln2_root(t, turn):
                pool.wait_ge(mv2_made[t], turn.made)
                reciprocal_root(mv2[:, t, 1:2], var2[:, t:t + 1], rstd2[:, t:t + 1], var2_made[t], rstd2_made[t], turn.made, 1)

            def normalise_probs(t, this):
                pool.wait_ge(inv_made[t], this.made)
                for half in range(2):
                    n = 2 * t + half
                    e = probs[:, t, half, :].rearrange("p (g k) -> p g k", k=SEQ)
                    nc.gpsimd.tensor_tensor(e, e, row_inv[:, t, half, :].unsqueeze(2).to_broadcast([P, 2 * HP, SEQ]),
                                            ALU.mult).then_inc(norm_made[n], 1)

            def shift(section, h, scaled, made, d, turn):
                pool.wait_ge(scaled, turn.made)
                at_b = slice(d * NB, (d + 1) * NB) if isinstance(d, int) else bass.ds(d * NB, NB)
                hv = h[:, :, :].rearrange("p c (b k) -> p c b k", b=NB)
                nc.gpsimd.tensor_tensor(hv, hv, mod_t[:, section, :, at_b].unsqueeze(3).to_broadcast([P, DC, NB, SEQ]),
                                        ALU.add).then_inc(made, 1)

            def gated_sum(t, buf, biased, gate, gated, addend, dst, made, turn):
                pool.wait_ge(biased[t], turn.made)
                nc.gpsimd.tensor_tensor(buf[:, t, :], buf[:, t, :], gate[:, t, :], ALU.mult).then_inc(gated[t], 1)
                pool.wait_ge(gated[t], turn.made)
                nc.gpsimd.tensor_tensor(dst[:, t, :], buf[:, t, :], addend[:, t, :], ALU.add).then_inc(made[t], 1)

            def step(s, has_prev=True, has_next=True):
                prev, this, nxt = turns(pool, s)
                fixed = isinstance(s, int)
                if has_next:
                    ln1_root(nxt)
                normalise_probs(0, this)
                if has_prev:
                    shift(SH2, h2, scaled2, h2_made, s - 1 if fixed else pool.snap(s - 1), prev)
                if has_next:
                    shift(SH1, h1, scaled1, h1_made, s + 1 if fixed else pool.snap(s + 1), nxt)
                normalise_probs(1, this)
                if has_prev:
                    pool.wait_ge(gate2_in, 32 * s if fixed else pool.snap(s * 32))
                    for t in range(TILES):
                        gated_sum(t, y_buf, y_biased, gate2, y_gated, x2, y_buf, y_made, prev)
                pool.wait_ge(gate1_in, 32 * (s + 1) if fixed else pool.snap(s * 32 + 32))
                pool.wait_ge(xres_in, 16 * (s + 1) if fixed else pool.snap(s * 16 + 16))
                for t in range(TILES):
                    gated_sum(t, o_buf, o_biased, gate1, o_gated, x_res, x2, x2_made, this)
                    ln2_root(t, this)

            nc.gpsimd.memset(ident[:, :], 0.0).then_inc(filled, 1)
            nc.gpsimd.memset(minus_half[:, :], -0.5).then_inc(filled, 1)
            nc.gpsimd.memset(eps[:, :], EPS).then_inc(filled, 1)
            pool.wait_ge(filled, 3)
            nc.gpsimd.affine_select(out=ident[:, :], in_=ident[:, :], compare_op=ALU.not_equal, fill=1.0,
                                    base=0, pattern=[[-1, P]], channel_multiplier=1).then_inc(ident_made, 1)
            first = Turn(1, 0)
            ln1_root(first)
            pool.wait_ge(mod_made, 4)
            shift(SH1, h1, scaled1, h1_made, 0, first)
            step(0, has_prev=False)
            with pool.Fori(1, STEPS - 1) as s:
                step(s)
            step(STEPS - 1, has_next=False)
            last = Turn(STEPS, STEPS - 1)
            shift(SH2, h2, scaled2, h2_made, STEPS - 1, last)
            pool.wait_ge(gate2_in, 32 * STEPS)
            for t in range(TILES):
                gated_sum(t, y_buf, y_biased, gate2, y_gated, x2, y_buf, y_made, last)


_INS = ['x', 'cond_1024', 'L0_cond_W_mod', 'L0_cond_b_mod', 'L0_cond_W_qkv', 'L0_cond_W_out', 'L0_cond_b_out',
        'L0_cond_W1', 'L0_cond_b1', 'L0_cond_W2', 'L0_cond_b2']


def kernel(**inputs):
    import numpy as _np
    import concourse.bacc as _bacc
    from concourse import mybir as _mybir
    from concourse.bass_utils import run_bass_kernel_spmd as _run

    nc = _bacc.Bacc("TRN2", target_bir_lowering=False, num_devices=1)
    arrays, args = {}, []
    for name in _INS:
        a = _np.ascontiguousarray(inputs[name])
        arrays[f"in_{name}_dram"] = a
        args.append(nc.dram_tensor(f"in_{name}_dram", a.shape, _mybir.dt.from_np(a.dtype), kind="ExternalInput").ap())
    args.append(nc.dram_tensor("out_0_dram", (BATCH, SEQ, DIM), _mybir.dt.float32, kind="ExternalOutput").ap())
    dit_block_kernel(nc, *args)
    r = _run(nc, [arrays], core_ids=[0])
    return r.results[0]["out_0_dram"]
```

```python
import concourse.bass as bass
from concourse import mybir
from contextlib import ExitStack

F32 = mybir.dt.float32
F32R = mybir.dt.float32r
ALU = mybir.AluOpType
ACT = mybir.ActivationFunctionType
AX = mybir.AxisListType

P = 128
BATCH, SEQ, DIM = 64, 64, 256
HEADS, DH = 16, 64
INNER = HEADS * DH
MLP = 1024
EPS = 1e-5
TILES = 2
TOK = TILES * P
NB = TOK // SEQ
STEPS = BATCH * SEQ // TOK
DC = DIM // P
PAIRS = HEADS // 2
MC = MLP // P
HALF = 512
HP = HALF // P
SH1, SC1, SH2, SC2 = range(4)


UNITS = ["v0", "v1", "v2", "ln2t", "v3", "ln1t", "ff1_0", "ff1_1", "ff1_2", "ff1_3", "qk0", "qk1", "qk2", "qk3",
         "ff2_0", "qk4", "o0", "qk5", "ff2_1", "qk6", "qk7", "o1"]
BANK = {unit: i % 3 for i, unit in enumerate(UNITS)}


class Turn:

    def __init__(self, made, before):
        self.made, self.before = made, before
        self.halves = None


def turns(engine, s):
    if isinstance(s, int):
        counts = [s - 1, s, s + 1, s + 2]
    else:
        counts = [engine.snap(s - 1), s, engine.snap(s + 1), engine.snap(s + 2)]
    return [Turn(counts[i + 1], counts[i]) for i in range(3)]


def count_halves(engine, s, this):
    this.halves = [2 * s + 1, 2 * s + 2] if isinstance(s, int) else [engine.snap(s * 2 + 1), engine.snap(s * 2 + 2)]


def hold(engine, sem, count):
    if not isinstance(count, int) or count > 0:
        engine.wait_ge(sem, count)


def apart(engine, passed, count):
    if not isinstance(count, int):
        engine.sem_inc(passed, 1)


def dit_block_kernel(nc, x, cond, w_mod, b_mod, w_qkv, w_out, b_out, w1, b1, w2, b2, out):
    ctx = ExitStack()
    with ctx:
        def sb(name, shape, dt=F32):
            return ctx.enter_context(nc.sbuf_tensor(name, shape, dt))

        def sem(name):
            return ctx.enter_context(nc.semaphore(name))

        def sems(name, n):
            return [sem(f"{name}{i}") for i in range(n)]

        wqkv_hi, wqkv_lo = (sb(f"wqkv_{k}", [P, DC, 3 * INNER], F32R) for k in ("hi", "lo"))
        wout_hi, wout_lo = (sb(f"wout_{k}", [P, PAIRS, DIM], F32R) for k in ("hi", "lo"))
        w1_hi, w1_lo = (sb(f"w1_{k}", [P, DC, MLP], F32R) for k in ("hi", "lo"))
        w2_hi, w2_lo = (sb(f"w2_{k}", [P, MC, DIM], F32R) for k in ("hi", "lo"))
        qk = sb("qk", [P, 2 * PAIRS, TOK])
        v = sb("v", [P, TILES, INNER])
        probs = sb("probs", [P, TILES, 2, HALF])
        probs_t = sb("probs_t", [P, 2, HP, 2, 2, SEQ])
        gelu = sb("gelu", [P, 2, HALF])
        att_hi, att_lo = (sb(f"att_{k}", [P, TILES, PAIRS, P], F32R) for k in ("hi", "lo"))
        g_hi, g_lo = (sb(f"g_{k}", [P, MC, TOK], F32R) for k in ("hi", "lo"))
        h1_hi, h1_lo = (sb(f"h1_{k}", [P, DC, TOK], F32R) for k in ("hi", "lo"))
        h2_hi, h2_lo = (sb(f"h2_{k}", [P, DC, TOK], F32R) for k in ("hi", "lo"))
        h1 = sb("h1", [P, DC, TOK])
        h2 = sb("h2", [P, DC, TOK])
        x_ln, xn1, x_res, xn2, gate1, gate2, o_buf, x2, y_buf = (
            sb(n, [P, TILES, DIM]) for n in
            ("x_ln", "xn1", "x_res", "xn2", "gate1", "gate2", "o_buf", "x2", "y_buf"))
        x2_last = xn1
        bout_bc = sb("bout_bc", [P, DIM])
        b2_bc = sb("b2_bc", [P, DIM])
        b1_col = sb("b1_col", [P, MC])
        mod_t = sb("mod_t", [P, 4, DC, BATCH])
        ident = sb("ident", [P, P])
        ones = sb("ones", [1, BATCH])
        minus_half = sb("minus_half", [P, TILES])
        eps = sb("eps", [P, TILES])
        stats1 = sb("stats1", [P, TILES, 6])
        stats2 = sb("stats2", [P, TILES, 6])
        mv1 = sb("mv1", [P, TILES, 2])
        mv2 = sb("mv2", [P, TILES, 2])
        rstd1 = sb("rstd1", [P, TILES])
        rstd2 = sb("rstd2", [P, TILES])
        var1 = sb("var1", [P, TILES])
        var2 = sb("var2", [P, TILES])
        row_max = sb("row_max", [P, TILES, 2, 2 * HP])
        row_sum = sb("row_sum", [P, TILES, 2, 2 * HP])
        row_inv = sb("row_inv", [P, TILES, 2, 2 * HP])
        wmod = qk[:, :, :].rearrange("p a b -> p (a b)")[:, 0:DC * 6 * DIM].rearrange("p (c n) -> p c n", c=DC)
        c_in, c_exp = x2[0:BATCH, 0, :], x2[0:BATCH, 1, :]
        silu = o_buf[0:BATCH, 0, :]
        silu_t = o_buf[:, 1, 0:DC * BATCH].rearrange("p (c b) -> p c b", c=DC)
        gates = y_buf[0:BATCH, :, :]
        bmod_row = probs_t[0:1].rearrange("p a i h b q -> p (a i h b q)")[:, 0:6 * DIM]
        stage = [v[:, :, :].rearrange("p t n -> p (t n)"),
                 probs[:, :, :, :].rearrange("p t a n -> p (t a n)"),
                 probs_t[:].rearrange("p a i h b q -> p (a i h b q)")]
        gate_rows = nc.dram_tensor("gate_rows", (BATCH, 2, DIM), F32, kind="Internal").ap()

        dense = [ctx.enter_context(nc.psum_tensor(f"dense{i}", [P, 2, TOK], F32)) for i in range(3)]
        s_ps = [ctx.enter_context(nc.psum_tensor(f"scores{i}", [P, HALF], F32)) for i in range(2)]
        pt_ps = ctx.enter_context(nc.psum_tensor("probs_t_ps", [P, HALF], F32))
        av_ps = [ctx.enter_context(nc.psum_tensor(f"att{i}", [P, HALF], F32)) for i in range(2)]

        cond_in, wmod_in, consts_in = sem("cond_in"), sem("wmod_in"), sem("consts_in")
        stage_in, w_hi_made, w_lo_made = sems("stage_in", 3), sem("w_hi_made"), sem("w_lo_made")
        filled, ident_made, ones_made = sem("filled"), sem("ident_made"), sem("ones_made")
        c_exp_made, silu_step, silu_t_ps = sem("c_exp_made"), sem("silu_step"), sem("silu_t_ps")
        silu_t_made, mod_ps, mod_made, gates_made = sem("silu_t_made"), sem("mod_ps"), sem("mod_made"), sem("gates_made")
        x_in, xres_in, gate1_in, gate2_in, stored = (sem(n) for n in ("x_in", "xres_in", "gate1_in", "gate2_in", "stored"))
        s_done, v_done, pt_done, av_done = sems("s_done", 4), sems("v_done", 4), sems("pt_done", 4), sems("av_done", 4)
        ln1t_done, ln2t_done = sem("ln1t_done"), sem("ln2t_done")
        qk_done, ff1_done, ff2_done, o_done = sems("qk_done", 8), sems("ff1_done", 4), sems("ff2_done", 2), sems("o_done", 2)
        pe_passed, dve_passed = sem("pe_passed"), sem("dve_passed")
        exp_made, v_made, pt_made, att_hi_made = sems("exp_made", 4), sems("v_made", 4), sems("pt_made", 4), sems("att_hi_made", 4)
        qk_made, gelu_made = sems("qk_made", 8), sems("gelu_made", 4)
        h1_hi_made, h2_hi_made = sem("h1_hi_made"), sem("h2_hi_made")
        max_made, sub_made, sum_made, inv_made = sems("max_made", 2), sems("sub_made", 4), sems("sum_made", 2), sems("inv_made", 2)
        scaled1, scaled2, h1_lo_made, h2_lo_made = sem("scaled1"), sem("scaled2"), sem("h1_lo_made"), sem("h2_lo_made")
        stats1_made, stats2_made = sems("stats1_made", 2), sems("stats2_made", 2)
        mv1_made, mv2_made, xn1_made, xn2_made = sem("mv1_made"), sems("mv2_made", 2), sems("xn1_made", 2), sems("xn2_made", 2)
        g_hi_made, g_lo_made, att_lo_made = sems("g_hi_made", 4), sems("g_lo_made", 4), sems("att_lo_made", 4)
        o_biased, y_biased = sems("o_biased", 2), sems("y_biased", 2)
        var1_made, rstd1_made, var2_made, rstd2_made = sem("var1_made"), sem("rstd1_made"), sems("var2_made", 2), sems("rstd2_made", 2)
        norm_made, h1_made, h2_made = sems("norm_made", 4), sem("h1_made"), sem("h2_made")
        o_gated, x2_made, y_gated, y_made = sems("o_gated", 2), sems("x2_made", 2), sems("y_gated", 2), sems("y_made", 2)

        x_v = x.rearrange("b q d -> (b q) d").rearrange("(s t p) d -> s p t d", t=TILES, p=P)
        out_v = out.rearrange("b q d -> (b q) d").rearrange("(s t p) d -> s p t d", t=TILES, p=P)
        gates_v = gate_rows.rearrange("(s t b) g d -> s b g t d", t=TILES, b=2)


        block = ctx.enter_context(nc.Block())

        @block.sync
        def _(sp):
            sp.dma_start(c_in, cond).then_inc(cond_in, 16)
            sp.dma_start(bmod_row, b_mod.rearrange("(o n) -> o n", o=1)).then_inc(wmod_in, 16)
            sp.dma_start(wmod, w_mod.rearrange("(c p) n -> p c n", p=P)).then_inc(wmod_in, 16)

            def load_x(d, turn):
                hold(sp, xn1_made[1], turn.before)
                src = x_v[d] if isinstance(d, int) else x_v[bass.ds(d, 1), :, :, :].squeeze(0)
                sp.dma_start(x_ln[:, :, :], src).then_inc(x_in, 16)

            def load_res(d, turn):
                hold(sp, x2_made[1], turn.before)
                src = x_v[d] if isinstance(d, int) else x_v[bass.ds(d, 1), :, :, :].squeeze(0)
                sp.dma_start(x_res[:, :, :], src).then_inc(xres_in, 16)
                load_gate(gate1, 0, d, gate1_in)

            def load_gate(tile, g, d, loaded):
                for b in range(2):
                    src = gates_v[d, b, g] if isinstance(d, int) else gates_v[bass.ds(d, 1), b, g, :, :].squeeze(0)
                    sp.dma_start(tile[SEQ * b:SEQ * (b + 1), :, :], src.partition_broadcast(SEQ)).then_inc(loaded, 16)

            def finish(d, turn):
                sp.wait_ge(y_made[0], turn.made)
                sp.wait_ge(y_made[1], turn.made)
                dst = out_v[d] if isinstance(d, int) else out_v[bass.ds(d, 1), :, :, :].squeeze(0)
                sp.dma_start(dst, y_buf[:, :, :]).then_inc(stored, 16)

            load_x(0, Turn(1, 0))
            wq_v = w_qkv.rearrange("(c p) n -> p c n", p=P)
            sources = [wq_v[:, :, 0:INNER], wq_v[:, :, INNER:2 * INNER], wq_v[:, :, 2 * INNER:3 * INNER],
                       w_out.rearrange("(c p) n -> p c n", p=P), w1.rearrange("(c p) n -> p c n", p=P),
                       w2.rearrange("(c p) n -> p c n", p=P)]
            for i, src in enumerate(sources):
                if i == 2:
                    sp.wait_ge(mod_ps, 2)
                if i >= 3:
                    sp.wait_ge(w_hi_made, i - 2)
                    sp.wait_ge(w_lo_made, i - 2)
                sp.dma_start(stage[i % 3].rearrange("p (c n) -> p c n", c=src.shape[1]), src).then_inc(stage_in[i % 3], 16)
                if i == 1:
                    sp.dma_start(bout_bc[:, :], b_out.partition_broadcast(P)).then_inc(consts_in, 16)
                    sp.dma_start(b2_bc[:, :], b2.partition_broadcast(P)).then_inc(consts_in, 16)
                    sp.dma_start(b1_col[:, :], b1.rearrange("(m p) -> p m", p=P),
                                 allow_slow_non_contiguous=True).then_inc(consts_in, 16)
                    sp.wait_ge(gates_made, 1)
                    sp.dma_start(gate_rows, gates).then_inc(stored, 16)
                if i == 2:
                    load_x(1, Turn(2, 1))
            sp.wait_ge(stored, 16)
            load_res(0, Turn(1, 0))
            load_gate(gate2, 1, 0, gate2_in)

            def step(s, has_next=True):
                prev, this, nxt = turns(sp, s)
                if has_next:
                    load_x(s + 1 if isinstance(s, int) else sp.snap(s + 1), nxt)
                load_res(s, this)
                finish(s - 1 if isinstance(s, int) else sp.snap(s - 1), prev)
                load_gate(gate2, 1, s, gate2_in)

            with sp.Fori(1, STEPS - 1) as s:
                step(s)
            step(STEPS - 1, has_next=False)
            finish(STEPS - 1, Turn(STEPS, STEPS - 1))
            sp.wait_ge(stored, 16 * (STEPS + 1))

        @block.tensor
        def _(pe):
            drained = {}

            def three_products(ps, terms, done=None):
                n = len(terms)
                for i, (a_hi, a_lo, b_hi, b_lo) in enumerate(terms):
                    pe_mm(ps, a_hi, b_hi, i == 0, False)
                    pe_mm(ps, a_hi, b_lo, False, False)
                    last = pe_mm(ps, a_lo, b_hi, False, i == n - 1)
                if done is not None:
                    last.then_inc(done, 1)

            def pe_mm(ps, a, b, start, stop):
                return nc.tensor.matmul(ps, a, b, start=start, stop=stop)

            def scores(t, half, this):
                hold(pe, sub_made[2 * (1 - t) + half], this.before if t == 0 else this.made)
                if half == 0 and t == 0:
                    for u in range(8):
                        pe.wait_ge(qk_made[u], this.made)
                apart(pe, pe_passed, this.made)
                for i in range(HP):
                    pair = HP * half + i
                    for b in range(2):
                        tok = slice(t * P + b * SEQ, t * P + (b + 1) * SEQ)
                        for h in range(2):
                            rows = slice(DH * h, DH * (h + 1))
                            last = pe_mm(s_ps[half][rows, i * P + b * SEQ:i * P + (b + 1) * SEQ],
                                         qk[rows, pair, tok], qk[rows, PAIRS + pair, tok], True, True)
                last.then_inc(s_done[2 * t + half], 1)

            def values(u, this):
                t, n = divmod(u, 2)
                bank = BANK[f"v{u}"]
                hold(pe, *drained[bank])
                if u == 0:
                    pe.wait_ge(h1_hi_made, this.made)
                    pe.wait_ge(h1_lo_made, this.made)
                tok, cols = slice(t * P, (t + 1) * P), slice(2 * INNER + n * HALF, 2 * INNER + (n + 1) * HALF)
                three_products(dense[bank][:, :, :].rearrange("p a b -> p (a b)"),
                               [(h1_hi[:, c, tok], h1_lo[:, c, tok], wqkv_hi[:, c, cols], wqkv_lo[:, c, cols])
                                for c in range(DC)], v_done[u])
                drained[bank] = (v_made[u], this.made)

            def transposed(xn, unit, made, done, drain, turn):
                bank = BANK[unit]
                hold(pe, *drained[bank])
                pe.wait_ge(made[0], turn.made)
                pe.wait_ge(made[1], turn.made)
                for t in range(TILES):
                    for c in range(DC):
                        last = nc.tensor.transpose(dense[bank][:, c, t * P:(t + 1) * P], xn[:, t, c * P:(c + 1) * P], ident[:, :])
                last.then_inc(done, 1)
                drained[bank] = (drain, turn.made)

            def ff1(u, prev):
                bank = BANK[f"ff1_{u}"]
                hold(pe, *drained[bank])
                if u == 0:
                    pe.wait_ge(h2_hi_made, prev.made)
                    pe.wait_ge(h2_lo_made, prev.made)
                for j in range(2):
                    cols = slice((2 * u + j) * P, (2 * u + j + 1) * P)
                    three_products(dense[bank][:, j, :],
                                   [(w1_hi[:, c, cols], w1_lo[:, c, cols], h2_hi[:, c, :], h2_lo[:, c, :])
                                    for c in range(DC)], ff1_done[u] if j == 1 else None)
                drained[bank] = (gelu_made[u], prev.made)

            def project_qk(u, nxt):
                bank = BANK[f"qk{u}"]
                hold(pe, *drained[bank])
                if u == 0:
                    pe.wait_ge(h1_hi_made, nxt.made)
                    pe.wait_ge(h1_lo_made, nxt.made)
                for j in range(2):
                    cols = slice((2 * u + j) * P, (2 * u + j + 1) * P)
                    three_products(dense[bank][:, j, :],
                                   [(wqkv_hi[:, c, cols], wqkv_lo[:, c, cols], h1_hi[:, c, :], h1_lo[:, c, :])
                                    for c in range(DC)], qk_done[u] if j == 1 else None)
                drained[bank] = (qk_made[u], nxt.made)

            def transpose_probs(t, half, this):
                n = 2 * t + half
                hold(pe, pt_made[(n - 1) % 4], this.before if n == 0 else this.made)
                pe.wait_ge(norm_made[n], this.made)
                for i in range(HP):
                    last = nc.tensor.transpose(pt_ps[:, i * P:(i + 1) * P], probs[:, t, half, i * P:(i + 1) * P], ident[:, :])
                last.then_inc(pt_done[n], 1)

            def attend(t, half, this):
                if t == 0 and half == 0:
                    for u in range(4):
                        pe.wait_ge(v_made[u], this.made)
                hold(pe, att_lo_made[2 * (1 - t) + half], this.before if t == 0 else this.made)
                pe.wait_ge(pt_made[2 * t + half], this.made)
                apart(pe, pe_passed, this.made)
                for i in range(HP):
                    for h in range(2):
                        head = 2 * (HP * half + i) + h
                        last = pe_mm(av_ps[half][DH * h:DH * (h + 1), i * P:(i + 1) * P],
                                     v[:, t, head * DH:(head + 1) * DH],
                                     probs_t[:, half, i, h, :, :].rearrange("p b q -> p (b q)"), True, True)
                last.then_inc(av_done[2 * t + half], 1)

            def project_out(t, this):
                bank = BANK[f"o{t}"]
                hold(pe, *drained[bank])
                for half in range(2):
                    pe.wait_ge(att_hi_made[2 * t + half], this.made)
                    pe.wait_ge(att_lo_made[2 * t + half], this.made)
                three_products(dense[bank][:, 0, :],
                               [(att_hi[:, t, c, :], att_lo[:, t, c, :], wout_hi[:, c, :], wout_lo[:, c, :])
                                for c in range(PAIRS)], o_done[t])
                drained[bank] = (o_biased[t], this.made)

            def ff2(t, prev):
                bank = BANK[f"ff2_{t}"]
                hold(pe, *drained[bank])
                if t == 0:
                    for u in range(4):
                        pe.wait_ge(g_hi_made[u], prev.made)
                        pe.wait_ge(g_lo_made[u], prev.made)
                tok = slice(t * P, (t + 1) * P)
                three_products(dense[bank][:, 0, :],
                               [(g_hi[:, m, tok], g_lo[:, m, tok], w2_hi[:, m, :], w2_lo[:, m, :])
                                for m in range(MC)], ff2_done[t])
                drained[bank] = (y_biased[t], prev.made)

            def step(s, has_prev=True, has_next=True):
                prev, this, nxt = turns(pe, s)
                if has_prev:
                    drained[BANK["o1"]] = (o_biased[1], prev.made)
                    drained[BANK["qk6"]], drained[BANK["qk7"]] = (qk_made[6], this.made), (qk_made[7], this.made)
                scores(0, 0, this)
                if not has_prev:
                    pe.wait_ge(w_hi_made, 6)
                    pe.wait_ge(w_lo_made, 6)
                values(0, this)
                scores(0, 1, this)
                values(1, this)
                values(2, this)
                if has_prev:
                    transposed(xn2, "ln2t", xn2_made, ln2t_done, scaled2, prev)
                values(3, this)
                scores(1, 0, this)
                transpose_probs(0, 0, this)
                if has_next:
                    transposed(xn1, "ln1t", xn1_made, ln1t_done, scaled1, nxt)
                scores(1, 1, this)
                transpose_probs(0, 1, this)
                if has_prev:
                    ff1(0, prev)
                else:
                    pe.wait_ge(filled, 5)
                attend(0, 0, this)
                if has_prev:
                    ff1(1, prev)
                attend(0, 1, this)
                if has_prev:
                    ff1(2, prev)
                    ff1(3, prev)
                if has_next:
                    project_qk(0, nxt)
                    project_qk(1, nxt)
                transpose_probs(1, 0, this)
                if has_next:
                    project_qk(2, nxt)
                transpose_probs(1, 1, this)
                if has_next:
                    project_qk(3, nxt)
                if has_prev and has_next:
                    ff2(0, prev)
                attend(1, 0, this)
                if has_next:
                    project_qk(4, nxt)
                project_out(0, this)
                attend(1, 1, this)
                if has_next:
                    project_qk(5, nxt)
                    if has_prev:
                        ff2(1, prev)
                    project_qk(6, nxt)
                    project_qk(7, nxt)
                project_out(1, this)
                if not has_next:
                    ff2(0, prev)
                    ff2(1, prev)

            pe.wait_ge(ident_made, 1)
            pe.wait_ge(ones_made, 1)
            pe.wait_ge(silu_step, 3)
            for c in range(DC):
                last = nc.tensor.transpose(s_ps[0][:, c * BATCH:(c + 1) * BATCH], silu[:, c * P:(c + 1) * P], ident[0:BATCH, 0:BATCH])
            last.then_inc(silu_t_ps, 1)
            pe.wait_ge(silu_t_made, 1)
            pe.wait_ge(wmod_in, 32)
            for k, section in enumerate((0, 1, 3, 4)):
                for c in range(DC):
                    cols = slice(section * DIM + c * P, section * DIM + (c + 1) * P)
                    ps = av_ps[0][:, (k * DC + c) * BATCH:(k * DC + c + 1) * BATCH]
                    for kc in range(DC):
                        pe_mm(ps, wmod[:, kc, cols], silu_t[:, kc, :], kc == 0, False)
                    last = pe_mm(ps, bmod_row[:, cols], ones[:, :], False, True)
            last.then_inc(mod_ps, 1)
            for g, section in enumerate((2, 5)):
                cols = slice(section * DIM, (section + 1) * DIM)
                ps = av_ps[1][0:BATCH, g * DIM:(g + 1) * DIM]
                for kc in range(DC):
                    pe_mm(ps, silu_t[:, kc, :], wmod[:, kc, cols], kc == 0, False)
                last = pe_mm(ps, ones[:, :], bmod_row[:, cols], False, True)
            last.then_inc(mod_ps, 1)

            first = Turn(1, 0)
            drained.update({b: (mod_ps, 0) for b in range(3)})
            transposed(xn1, "ln1t", xn1_made, ln1t_done, scaled1, first)
            pe.wait_ge(w_hi_made, 2)
            pe.wait_ge(w_lo_made, 2)
            for u in range(8):
                project_qk(u, first)
            step(0, has_prev=False)
            with pe.Fori(1, STEPS - 1) as s:
                step(s)
            step(STEPS - 1, has_next=False)
            last = Turn(STEPS, STEPS - 1)
            transposed(xn2, "ln2t", xn2_made, ln2t_done, scaled2, last)
            for u in range(4):
                ff1(u, last)
            ff2(0, last)
            ff2(1, last)

        @block.scalar
        def _(act):
            def copy_bank(dst, src, made):
                nc.scalar.activation(dst, src, ACT.Copy).then_inc(made, 1)

            def high_part(dst, src, whole_made, made, turn):
                act.wait_ge(whole_made, turn.made)
                nc.scalar.activation(dst[:, :, :], src[:, :, :], ACT.Copy).then_inc(made, 1)

            def flat(ps):
                return ps[:, :, :].rearrange("p a b -> p (a b)")

            def exp(t, half, this):
                n = 2 * t + half
                act.wait_ge(sub_made[n], this.made)
                e = probs[:, t, half, :]
                nc.scalar.activation(e, e, ACT.Exp, scale=DH ** -0.5).then_inc(exp_made[n], 1)

            def take_v(u, this):
                act.wait_ge(v_done[u], this.made)
                t, n = divmod(u, 2)
                copy_bank(v[:, t, n * HALF:(n + 1) * HALF], flat(dense[BANK[f"v{u}"]]), v_made[u])

            def take_qk(u, nxt):
                act.wait_ge(qk_done[u], nxt.made)
                bank = BANK[f"qk{u}"]
                copy_bank(qk[:, 2 * u:2 * u + 2, :], dense[bank][:, :, :], qk_made[u])

            def gelus(u, prev):
                act.wait_ge(ff1_done[u], prev.made)
                if u >= 2:
                    act.wait_ge(g_lo_made[u - 2], prev.made)
                for j in range(2):
                    m = 2 * u + j
                    last = nc.scalar.activation(gelu[:, u % 2, j * TOK:(j + 1) * TOK], dense[BANK[f"ff1_{u}"]][:, j, :], ACT.Gelu,
                                                bias=b1_col[:, m:m + 1])
                last.then_inc(gelu_made[u], 1)

            def take_pt(t, half, this):
                n = 2 * t + half
                act.wait_ge(pt_done[n], this.made)
                for b in range(2):
                    rows = slice(SEQ * b, SEQ * (b + 1))
                    last = nc.scalar.activation(probs_t[rows, half, :, :, b, :],
                                                pt_ps[rows, :].rearrange("p (i h q) -> p i h q", i=HP, h=2), ACT.Copy)
                last.then_inc(pt_made[n], 1)

            def att_high(t, half, this):
                n = 2 * t + half
                act.wait_ge(av_done[n], this.made)
                copy_bank(att_hi[:, t, HP * half:HP * (half + 1), :], av_ps[half][:, :].rearrange("p (i q) -> p i q", i=HP),
                          att_hi_made[n])

            def step(s, has_prev=True, has_next=True):
                prev, this, nxt = turns(act, s)
                if not has_prev:
                    act.wait_ge(w_lo_made, 6)
                take_v(0, this)
                exp(0, 0, this)
                take_v(1, this)
                exp(0, 1, this)
                take_v(2, this)
                take_v(3, this)
                if has_prev:
                    high_part(h2_hi, h2, h2_made, h2_hi_made, prev)
                take_pt(0, 0, this)
                exp(1, 0, this)
                take_pt(0, 1, this)
                exp(1, 1, this)
                if has_prev:
                    gelus(0, prev)
                if has_next:
                    high_part(h1_hi, h1, h1_made, h1_hi_made, nxt)
                if has_prev:
                    gelus(1, prev)
                att_high(0, 0, this)
                if has_prev:
                    gelus(2, prev)
                att_high(0, 1, this)
                if has_prev:
                    gelus(3, prev)
                if has_next:
                    take_qk(0, nxt)
                    take_qk(1, nxt)
                take_pt(1, 0, this)
                if has_next:
                    take_qk(2, nxt)
                take_pt(1, 1, this)
                if has_next:
                    take_qk(3, nxt)
                att_high(1, 0, this)
                if has_next:
                    take_qk(4, nxt)
                att_high(1, 1, this)
                if has_next:
                    take_qk(5, nxt)
                    take_qk(6, nxt)
                    take_qk(7, nxt)

            act.wait_ge(cond_in, 16)
            nc.scalar.activation(c_exp, c_in, ACT.Exp, scale=-1.0).then_inc(c_exp_made, 1)
            act.wait_ge(silu_t_ps, 1)
            copy_bank(silu_t, s_ps[0][:, 0:DC * BATCH].rearrange("p (c b) -> p c b", c=DC), silu_t_made)
            act.wait_ge(mod_ps, 2)
            copy_bank(gates, av_ps[1][0:BATCH, :].rearrange("p (g d) -> p g d", g=2), gates_made)
            first = Turn(1, 0)
            targets = [wqkv_hi[:, :, 0:INNER], wqkv_hi[:, :, INNER:2 * INNER], wqkv_hi[:, :, 2 * INNER:], wout_hi, w1_hi, w2_hi]

            def split_weights(i):
                act.wait_ge(stage_in[i % 3], 16 * (i // 3 + 1))
                dst = targets[i][:, :, :]
                nc.scalar.activation(dst, stage[i % 3].rearrange("p (c n) -> p c n", c=dst.shape[1]), ACT.Copy).then_inc(w_hi_made, 1)

            split_weights(0)
            split_weights(1)
            high_part(h1_hi, h1, h1_made, h1_hi_made, first)
            for i in range(2, 6):
                split_weights(i)
                take_qk(2 * (i - 2), first)
                take_qk(2 * (i - 2) + 1, first)
            act.wait_ge(consts_in, 48)
            step(0, has_prev=False)
            with act.Fori(1, STEPS - 1) as s:
                step(s)
            step(STEPS - 1, has_next=False)
            last = Turn(STEPS, STEPS - 1)
            high_part(h2_hi, h2, h2_made, h2_hi_made, last)
            for u in range(4):
                gelus(u, last)

        @block.vector
        def _(dve):
            def heads(ap):
                return ap.rearrange("p (g k) -> p g k", k=SEQ)

            def by_row(ap):
                return ap.unsqueeze(2).to_broadcast([P, 2 * HP, SEQ])

            def maxima(t, half, this):
                n = 2 * t + half
                dve.wait_ge(s_done[n], this.made)
                nc.vector.tensor_reduce(row_max[:, t, half, :], heads(s_ps[half][:, :]), AX.X, ALU.max).then_inc(max_made[t], 1)

            def subtract(t, half, this):
                n = 2 * t + half
                dve.wait_ge(max_made[t], this.halves[half])
                nc.vector.tensor_tensor(heads(probs[:, t, half, :]), heads(s_ps[half][:, :]), by_row(row_max[:, t, half, :]),
                                        ALU.subtract).then_inc(sub_made[n], 1)

            def sums(t, half, this):
                n = 2 * t + half
                dve.wait_ge(exp_made[n], this.made)
                nc.vector.tensor_reduce(row_sum[:, t, half, :], heads(probs[:, t, half, :]), AX.X, ALU.add).then_inc(sum_made[t], 1)
                dve.wait_ge(sum_made[t], this.halves[half])
                nc.vector.reciprocal(row_inv[:, t, half, :], row_sum[:, t, half, :]).then_inc(inv_made[t], 1)

            def row_stats(src, t, stats, mv, stats_made, mv_done, turn):
                nc.vector.bn_stats(stats[:, t, :], src[:, t, :]).then_inc(stats_made[t], 1)
                dve.wait_ge(stats_made[t], turn.made)
                apart(dve, dve_passed, turn.made)
                last = nc.vector.bn_aggr(mv[:, t, :], stats[:, t, :])
                if mv_done is not None:
                    last.then_inc(mv_done, 1)

            def normalise(src, t, mv, rstd, dst, made):
                nc.vector.tensor_scalar(dst[:, t, :], src[:, t, :], mv[:, t, 0:1], rstd[:, t:t + 1],
                                        ALU.subtract, ALU.mult).then_inc(made[t], 1)

            def ln1_stats(d, turn, loaded):
                dve.wait_ge(x_in, loaded)
                for t in range(TILES):
                    row_stats(x_ln, t, stats1, mv1, stats1_made, mv1_made if t == 1 else None, turn)

            def ln1_rows(turn):
                dve.wait_ge(rstd1_made, turn.made)
                for t in range(TILES):
                    normalise(x_ln, t, mv1, rstd1, xn1, xn1_made)

            def scale(unit, section, h, done, made, d, turn):
                dve.wait_ge(done, turn.made)
                at_b = slice(d * NB, (d + 1) * NB) if isinstance(d, int) else bass.ds(d * NB, NB)
                nc.vector.tensor_tensor(h[:, :, :].rearrange("p c (b k) -> p c b k", b=NB),
                                        dense[BANK[unit]][:, :, :].rearrange("p c (b k) -> p c b k", b=NB),
                                        mod_t[:, section, :, at_b].unsqueeze(3).to_broadcast([P, DC, NB, SEQ]),
                                        ALU.mult).then_inc(made, 1)

            def low_part(lo, src, hi, hi_made, made, turn):
                dve.wait_ge(hi_made, turn.made)
                nc.vector.tensor_tensor(lo[:, :, :], src[:, :, :], hi[:, :, :].bitcast(F32), ALU.subtract).then_inc(made, 1)

            def split_gelu(u, prev):
                dve.wait_ge(gelu_made[u], prev.made)
                g = gelu[:, u % 2, :].rearrange("p (a b) -> p a b", a=2)
                hi, lo = g_hi[:, 2 * u:2 * u + 2, :], g_lo[:, 2 * u:2 * u + 2, :]
                nc.vector.tensor_copy(hi, g).then_inc(g_hi_made[u], 1)
                dve.wait_ge(g_hi_made[u], prev.made)
                nc.vector.tensor_tensor(lo, g, hi.bitcast(F32), ALU.subtract).then_inc(g_lo_made[u], 1)

            def att_low(t, half, this):
                n = 2 * t + half
                dve.wait_ge(att_hi_made[n], this.made)
                pairs = slice(HP * half, HP * (half + 1))
                nc.vector.tensor_tensor(att_lo[:, t, pairs, :], av_ps[half][:, :].rearrange("p (i q) -> p i q", i=HP),
                                        att_hi[:, t, pairs, :].bitcast(F32), ALU.subtract).then_inc(att_lo_made[n], 1)

            def add_bias(t, unit, done, bias, dst, made, turn):
                dve.wait_ge(done[t], turn.made)
                nc.vector.tensor_tensor(dst[:, t, :], dense[BANK[unit]][:, 0, :], bias[:, :], ALU.add).then_inc(made[t], 1)

            def ln2_stats(t, this, rows=x2):
                dve.wait_ge(x2_made[t], this.made)
                row_stats(rows, t, stats2, mv2, stats2_made, mv2_made[t], this)

            def ln2_rows(t, this, rows=x2):
                dve.wait_ge(rstd2_made[t], this.made)
                normalise(rows, t, mv2, rstd2, xn2, xn2_made)

            def project_biased(t, this):
                add_bias(t, f"o{t}", o_done, bout_bc, o_buf, o_biased, this)

            def mlp_biased(t, prev, stores):
                if t == 0:
                    dve.wait_ge(stored, stores)
                add_bias(t, f"ff2_{t}", ff2_done, b2_bc, y_buf, y_biased, prev)

            def step(s, has_prev=True, has_next=True):
                prev, this, nxt = turns(dve, s)
                count_halves(dve, s, this)
                fixed = isinstance(s, int)
                stores = 16 * s if fixed else dve.snap(s * 16)
                maxima(0, 0, this)
                if has_prev:
                    ln2_stats(1, prev)
                subtract(0, 0, this)
                if has_prev:
                    ln2_rows(1, prev)
                maxima(0, 1, this)
                subtract(0, 1, this)
                if has_next:
                    ln1_stats(None, nxt, 16 * (s + 2) if fixed else dve.snap(s * 16 + 32))
                sums(0, 0, this)
                if has_prev:
                    scale("ln2t", SC2, h2, ln2t_done, scaled2, s - 1 if fixed else dve.snap(s - 1), prev)
                sums(0, 1, this)
                if has_next:
                    ln1_rows(nxt)
                if has_prev:
                    low_part(h2_lo, h2, h2_hi, h2_hi_made, h2_lo_made, prev)
                maxima(1, 0, this)
                subtract(1, 0, this)
                if has_next:
                    scale("ln1t", SC1, h1, ln1t_done, scaled1, s + 1 if fixed else dve.snap(s + 1), nxt)
                maxima(1, 1, this)
                subtract(1, 1, this)
                sums(1, 0, this)
                if has_prev:
                    split_gelu(0, prev)
                if has_next:
                    low_part(h1_lo, h1, h1_hi, h1_hi_made, h1_lo_made, nxt)
                sums(1, 1, this)
                if has_prev:
                    split_gelu(1, prev)
                att_low(0, 0, this)
                if has_prev:
                    split_gelu(2, prev)
                att_low(0, 1, this)
                if has_prev:
                    split_gelu(3, prev)
                if has_prev and has_next:
                    mlp_biased(0, prev, stores)
                att_low(1, 0, this)
                project_biased(0, this)
                att_low(1, 1, this)
                new_x2 = x2 if has_next else x2_last
                ln2_stats(0, this, new_x2)
                ln2_rows(0, this, new_x2)
                if has_prev and has_next:
                    mlp_biased(1, prev, stores)
                project_biased(1, this)
                if not has_next:
                    ln2_stats(1, this, new_x2)
                    ln2_rows(1, this, new_x2)
                    mlp_biased(0, prev, stores)
                    mlp_biased(1, prev, stores)

            nc.vector.memset(ones[:, :], 1.0).then_inc(ones_made, 1)
            dve.wait_ge(c_exp_made, 1)
            nc.vector.tensor_scalar(c_exp, c_exp, 1.0, None, ALU.add).then_inc(silu_step, 1)
            dve.wait_ge(silu_step, 1)
            nc.vector.reciprocal(c_exp, c_exp).then_inc(silu_step, 1)
            dve.wait_ge(silu_step, 2)
            nc.vector.tensor_tensor(silu, c_in, c_exp, ALU.mult).then_inc(silu_step, 1)
            first, second = Turn(1, 0), Turn(2, 1)
            ln1_stats(0, first, 16)
            ln1_rows(first)
            dve.wait_ge(mod_ps, 1)
            for k in range(4):
                ps = av_ps[0][:, k * DC * BATCH:(k + 1) * DC * BATCH].rearrange("p (c b) -> p c b", c=DC)
                if k in (SC1, SC2):
                    nc.vector.tensor_scalar(mod_t[:, k, :, :], ps, 1.0, None, ALU.add).then_inc(mod_made, 1)
                else:
                    nc.vector.tensor_copy(mod_t[:, k, :, :], ps).then_inc(mod_made, 1)
            dve.wait_ge(mod_made, 4)
            targets = [(wqkv_hi[:, :, 0:INNER], wqkv_lo[:, :, 0:INNER]),
                       (wqkv_hi[:, :, INNER:2 * INNER], wqkv_lo[:, :, INNER:2 * INNER]),
                       (wqkv_hi[:, :, 2 * INNER:], wqkv_lo[:, :, 2 * INNER:]),
                       (wout_hi, wout_lo), (w1_hi, w1_lo), (w2_hi, w2_lo)]

            def split_weights(i):
                dve.wait_ge(w_hi_made, i + 1)
                hi, lo = (w[:, :, :] for w in targets[i])
                nc.vector.tensor_tensor(lo, stage[i % 3].rearrange("p (c n) -> p c n", c=hi.shape[1]), hi.bitcast(F32),
                                        ALU.subtract).then_inc(w_lo_made, 1)

            scale("ln1t", SC1, h1, ln1t_done, scaled1, 0, first)
            split_weights(0)
            split_weights(1)
            low_part(h1_lo, h1, h1_hi, h1_hi_made, h1_lo_made, first)
            for i in range(2, 6):
                split_weights(i)
            dve.wait_ge(consts_in, 48)
            step(0, has_prev=False)
            with dve.Fori(1, STEPS - 1) as s:
                step(s)
            step(STEPS - 1, has_next=False)
            last = Turn(STEPS, STEPS - 1)
            scale("ln2t", SC2, h2, ln2t_done, scaled2, STEPS - 1, last)
            low_part(h2_lo, h2, h2_hi, h2_hi_made, h2_lo_made, last)
            for u in range(4):
                split_gelu(u, last)
            mlp_biased(0, last, 16 * STEPS)
            mlp_biased(1, last, 16 * STEPS)

        @block.gpsimd
        def _(pool):
            def reciprocal_root(mv, var, rstd, var_done, rstd_done, count, width):
                nc.gpsimd.tensor_tensor(var, mv, eps[:, 0:width], ALU.add).then_inc(var_done, 1)
                pool.wait_ge(var_done, count)
                nc.gpsimd.tensor_tensor(rstd, var, minus_half[:, 0:width], ALU.pow).then_inc(rstd_done, 1)

            def ln1_root(turn):
                pool.wait_ge(mv1_made, turn.made)
                reciprocal_root(mv1[:, :, 1], var1[:, :], rstd1[:, :], var1_made, rstd1_made, turn.made, TILES)

            def ln2_root(t, turn):
                pool.wait_ge(mv2_made[t], turn.made)
                reciprocal_root(mv2[:, t, 1:2], var2[:, t:t + 1], rstd2[:, t:t + 1], var2_made[t], rstd2_made[t], turn.made, 1)

            def normalise_probs(t, half, this):
                pool.wait_ge(inv_made[t], this.halves[half])
                e = probs[:, t, half, :].rearrange("p (g k) -> p g k", k=SEQ)
                nc.gpsimd.tensor_tensor(e, e, row_inv[:, t, half, :].unsqueeze(2).to_broadcast([P, 2 * HP, SEQ]),
                                        ALU.mult).then_inc(norm_made[2 * t + half], 1)

            def shift(section, h, scaled, made, d, turn):
                pool.wait_ge(scaled, turn.made)
                at_b = slice(d * NB, (d + 1) * NB) if isinstance(d, int) else bass.ds(d * NB, NB)
                hv = h[:, :, :].rearrange("p c (b k) -> p c b k", b=NB)
                nc.gpsimd.tensor_tensor(hv, hv, mod_t[:, section, :, at_b].unsqueeze(3).to_broadcast([P, DC, NB, SEQ]),
                                        ALU.add).then_inc(made, 1)

            def gated_sum(t, buf, biased, gate, gated, addend, dst, made, turn):
                pool.wait_ge(biased[t], turn.made)
                nc.gpsimd.tensor_tensor(buf[:, t, :], buf[:, t, :], gate[:, t, :], ALU.mult).then_inc(gated[t], 1)
                pool.wait_ge(gated[t], turn.made)
                nc.gpsimd.tensor_tensor(dst[:, t, :], buf[:, t, :], addend[:, t, :], ALU.add).then_inc(made[t], 1)

            def mlp_sum(t, turn, rows=x2):
                gated_sum(t, y_buf, y_biased, gate2, y_gated, rows, y_buf, y_made, turn)

            def attention_sum(t, turn, rows=x2):
                gated_sum(t, o_buf, o_biased, gate1, o_gated, x_res, rows, x2_made, turn)

            def step(s, has_prev=True, has_next=True):
                prev, this, nxt = turns(pool, s)
                count_halves(pool, s, this)
                fixed = isinstance(s, int)
                if has_prev:
                    ln2_root(1, prev)
                if has_next:
                    ln1_root(nxt)
                normalise_probs(0, 0, this)
                if has_prev:
                    shift(SH2, h2, scaled2, h2_made, s - 1 if fixed else pool.snap(s - 1), prev)
                normalise_probs(0, 1, this)
                if has_next:
                    shift(SH1, h1, scaled1, h1_made, s + 1 if fixed else pool.snap(s + 1), nxt)
                normalise_probs(1, 0, this)
                normalise_probs(1, 1, this)
                if has_prev:
                    pool.wait_ge(gate2_in, 32 * s if fixed else pool.snap(s * 32))
                if has_prev and has_next:
                    mlp_sum(0, prev)
                pool.wait_ge(gate1_in, 32 * (s + 1) if fixed else pool.snap(s * 32 + 32))
                pool.wait_ge(xres_in, 16 * (s + 1) if fixed else pool.snap(s * 16 + 16))
                new_x2 = x2 if has_next else x2_last
                attention_sum(0, this, new_x2)
                ln2_root(0, this)
                if has_prev and has_next:
                    mlp_sum(1, prev)
                attention_sum(1, this, new_x2)
                if not has_next:
                    ln2_root(1, this)
                    mlp_sum(0, prev)
                    mlp_sum(1, prev)

            nc.gpsimd.memset(ident[:, :], 0.0).then_inc(filled, 1)
            nc.gpsimd.memset(minus_half[:, :], -0.5).then_inc(filled, 1)
            nc.gpsimd.memset(eps[:, :], EPS).then_inc(filled, 1)
            pool.wait_ge(filled, 3)
            nc.gpsimd.affine_select(out=ident[:, :], in_=ident[:, :], compare_op=ALU.not_equal, fill=1.0,
                                    base=0, pattern=[[-1, P]], channel_multiplier=1).then_inc(ident_made, 1)
            first = Turn(1, 0)
            ln1_root(first)
            pool.wait_ge(mod_made, 4)
            shift(SH1, h1, scaled1, h1_made, 0, first)
            pool.wait_ge(w_lo_made, 6)
            for b in range(2):
                nc.gpsimd.memset(probs_t[SEQ * b:SEQ * (b + 1), :, :, :, 1 - b, :], 0.0).then_inc(filled, 1)
            pool.wait_ge(filled, 5)
            step(0, has_prev=False)
            with pool.Fori(1, STEPS - 1) as s:
                step(s)
            step(STEPS - 1, has_next=False)
            last = Turn(STEPS, STEPS - 1)
            shift(SH2, h2, scaled2, h2_made, STEPS - 1, last)
            pool.wait_ge(gate2_in, 32 * STEPS)
            for t in range(TILES):
                mlp_sum(t, last, x2_last)


_INS = ['x', 'cond_1024', 'L0_cond_W_mod', 'L0_cond_b_mod', 'L0_cond_W_qkv', 'L0_cond_W_out', 'L0_cond_b_out',
        'L0_cond_W1', 'L0_cond_b1', 'L0_cond_W2', 'L0_cond_b2']


def kernel(**inputs):
    import numpy as _np
    import concourse.bacc as _bacc
    from concourse import mybir as _mybir
    from concourse.bass_utils import run_bass_kernel_spmd as _run

    nc = _bacc.Bacc("TRN2", target_bir_lowering=False, num_devices=1)
    arrays, args = {}, []
    for name in _INS:
        a = _np.ascontiguousarray(inputs[name])
        arrays[f"in_{name}_dram"] = a
        args.append(nc.dram_tensor(f"in_{name}_dram", a.shape, _mybir.dt.from_np(a.dtype), kind="ExternalInput").ap())
    args.append(nc.dram_tensor("out_0_dram", (BATCH, SEQ, DIM), _mybir.dt.float32, kind="ExternalOutput").ap())
    dit_block_kernel(nc, *args)
    r = _run(nc, [arrays], core_ids=[0])
    return r.results[0]["out_0_dram"]
```

```python
import concourse.bass as bass
from concourse import mybir
from contextlib import ExitStack

F32 = mybir.dt.float32
F32R = mybir.dt.float32r
ALU = mybir.AluOpType
ACT = mybir.ActivationFunctionType
AX = mybir.AxisListType

P = 128
BATCH, SEQ, DIM = 64, 64, 256
HEADS, DH = 16, 64
INNER = HEADS * DH
MLP = 1024
EPS = 1e-5
TILES = 2
TOK = TILES * P
NB = TOK // SEQ
STEPS = BATCH * SEQ // TOK
DC = DIM // P
PAIRS = HEADS // 2
MC = MLP // P
HALF = 512
HP = HALF // P
BLOCK = 32
SH1, SC1, SH2, SC2 = range(4)


UNITS = ["v0", "v1", "ln2t", "v2", "v3", "ln1t", "ff1_0", "ff1_1", "ff1_2", "ff1_3", "qk0", "qk1", "qk2", "qk3",
         "qk4", "qk5", "qk6", "ff2_0", "ff2_1", "o0", "qk7", "o1"]
BANK = {unit: i % 3 for i, unit in enumerate(UNITS)}
END_BANK = {"ln2t": 1, "ff1_0": 2, "ff1_1": 0, "ff1_2": 1, "ff1_3": 2, "ff2_0": 0, "ff2_1": 1}
LAST_BANK = {"o0": 1, "o1": 0, "ff2_0": 2, "ff2_1": 0}


class Turn:

    def __init__(self, made, before):
        self.made, self.before = made, before
        self.halves = None


def turns(engine, s):
    if isinstance(s, int):
        counts = [s - 1, s, s + 1, s + 2]
    else:
        counts = [engine.snap(s - 1), s, engine.snap(s + 1), engine.snap(s + 2)]
    return [Turn(counts[i + 1], counts[i]) for i in range(3)]


def count_halves(engine, s, this):
    this.halves = [2 * s + 1, 2 * s + 2] if isinstance(s, int) else [engine.snap(s * 2 + 1), engine.snap(s * 2 + 2)]


def hold(engine, sem, count):
    if not isinstance(count, int) or count > 0:
        engine.wait_ge(sem, count)


def apart(engine, passed, count):
    if not isinstance(count, int):
        engine.sem_inc(passed, 1)


def dit_block_kernel(nc, x, cond, w_mod, b_mod, w_qkv, w_out, b_out, w1, b1, w2, b2, out):
    ctx = ExitStack()
    with ctx:
        def sb(name, shape, dt=F32):
            return ctx.enter_context(nc.sbuf_tensor(name, shape, dt))

        def sem(name):
            return ctx.enter_context(nc.semaphore(name))

        def sems(name, n):
            return [sem(f"{name}{i}") for i in range(n)]

        wqkv_hi, wqkv_lo = (sb(f"wqkv_{k}", [P, DC, 3 * INNER], F32R) for k in ("hi", "lo"))
        wout_hi, wout_lo = (sb(f"wout_{k}", [P, PAIRS, DIM], F32R) for k in ("hi", "lo"))
        w1_hi, w1_lo = (sb(f"w1_{k}", [P, DC, MLP], F32R) for k in ("hi", "lo"))
        w2_hi, w2_lo = (sb(f"w2_{k}", [P, MC, DIM], F32R) for k in ("hi", "lo"))
        qk = sb("qk", [P, 2 * PAIRS, TOK])
        v = sb("v", [P, TILES, INNER])
        probs = sb("probs", [P, TILES, 2, HALF])
        probs_t = sb("probs_t", [P, 2, HP, 2, 2, SEQ])
        gelu = sb("gelu", [P, 2, HALF])
        att_hi, att_lo = (sb(f"att_{k}", [P, TILES, PAIRS, P], F32R) for k in ("hi", "lo"))
        g_hi, g_lo = (sb(f"g_{k}", [P, MC, TOK], F32R) for k in ("hi", "lo"))
        h1_hi, h1_lo = (sb(f"h1_{k}", [P, DC, TOK], F32R) for k in ("hi", "lo"))
        h2_hi, h2_lo = (sb(f"h2_{k}", [P, DC, TOK], F32R) for k in ("hi", "lo"))
        h1 = sb("h1", [P, DC, TOK])
        h2 = sb("h2", [P, DC, TOK])
        x_ln, xn1, x_res, xn2, gate1, gate2, o_buf, x2, y_buf = (
            sb(n, [P, TILES, DIM]) for n in
            ("x_ln", "xn1", "x_res", "xn2", "gate1", "gate2", "o_buf", "x2", "y_buf"))
        x2_last = xn1
        bout_bc = sb("bout_bc", [P, DIM])
        b2_bc = sb("b2_bc", [P, DIM])
        b1_col = sb("b1_col", [P, MC])
        mod_t = sb("mod_t", [P, 4, DC, BATCH])
        ident = sb("ident", [P, P])
        bmod_col = sb("bmod_col", [P, 6 * DC])
        minus_half = sb("minus_half", [P, TILES])
        eps = sb("eps", [P, TILES])
        stats1 = sb("stats1", [P, TILES, 6])
        stats2 = sb("stats2", [P, TILES, 6])
        mv1 = sb("mv1", [P, TILES, 2])
        mv2 = sb("mv2", [P, TILES, 2])
        rstd1 = sb("rstd1", [P, TILES])
        rstd2 = sb("rstd2", [P, TILES])
        var1 = sb("var1", [P, TILES])
        var2 = sb("var2", [P, TILES])
        row_max = sb("row_max", [P, TILES, 2, 2 * HP])
        row_sum = sb("row_sum", [P, TILES, 2, 2 * HP])
        row_inv = sb("row_inv", [P, TILES, 2, 2 * HP])
        wmod1, wmod2, wmod_g = (qk[:, i:i + 4, :].rearrange("p a b -> p (a b)").rearrange("p (c n) -> p c n", c=DC) for i in (0, 8, 12))
        c_in = x2[0:BATCH, 0, :]
        c_exp, silu_flat = (o_buf[:, i, 0:DC * BATCH] for i in range(2))
        silu_t = silu_flat.rearrange("p (c b) -> p c b", c=DC)
        gates, gate_bias = y_buf[0:BATCH, :, :], xn2[0:BATCH, :, :]
        stage_q, stage_k, stage_v = (ap.rearrange("p (c n) -> p c n", c=DC) for ap in (
            v[:, :, :].rearrange("p t n -> p (t n)"),
            probs[:, :, :, :].rearrange("p t a n -> p (t a n)"),
            probs_t[:].rearrange("p a i h b q -> p (a i h b q)")))
        small_stages = [gelu[:, 0, :], gelu[:, 1, :], h2[:, :, :].rearrange("p c n -> p (c n)")]
        gate_rows = nc.dram_tensor("gate_rows", (BATCH, 2, DIM), F32, kind="Internal").ap()

        dense = [ctx.enter_context(nc.psum_tensor(f"dense{i}", [P, 2, TOK], F32)) for i in range(3)]
        s_ps = [ctx.enter_context(nc.psum_tensor(f"scores{i}", [P, HALF], F32)) for i in range(2)]
        pt_ps = ctx.enter_context(nc.psum_tensor("probs_t_ps", [P, HALF], F32))
        av_ps = [ctx.enter_context(nc.psum_tensor(f"att{i}", [P, HALF], F32)) for i in range(2)]

        cond_in, bmod_in, wmod1_in, wmod2_in, gates_w_in, consts_in = sem("cond_in"), sem("gates_w_in"), sem("bmod_in"), sem("wmod1_in"), sem("wmod2_in"), sem("consts_in")
        stage_in, small_in, w_hi_made, w_lo_made = sems("stage_in", 3), sems("small_in", 3), sem("w_hi_made"), sem("w_lo_made")
        filled, ident_made, bias_made = sem("filled"), sem("ident_made"), sem("bias_made")
        c_exp_made, silu_step, c_t_done = sem("c_exp_made"), sem("silu_step"), sem("c_t_done")
        silu_t_made, mod_ps, mod_made, gates_made = sem("silu_t_made"), sem("mod_ps"), sem("mod_made"), sem("gates_made")
        x_in, xres_in, gate1_in, gate2_in, stored = (sem(n) for n in ("x_in", "xres_in", "gate1_in", "gate2_in", "stored"))
        s_done, v_done, pt_done, av_done = sems("s_done", 4), sems("v_done", 4), sems("pt_done", 4), sems("av_done", 4)
        ln1t_done, ln2t_done = sem("ln1t_done"), sem("ln2t_done")
        qk_done, ff1_done, ff2_done, o_done = sems("qk_done", 8), sems("ff1_done", 4), sems("ff2_done", 2), sems("o_done", 2)
        pe_passed, dve_passed = sem("pe_passed"), sem("dve_passed")
        exp_made, v_made, pt_made, att_hi_made = sems("exp_made", 4), sems("v_made", 4), sems("pt_made", 4), sems("att_hi_made", 4)
        qk_made, gelu_made = sems("qk_made", 8), sems("gelu_made", 4)
        h1_hi_made, h2_hi_made = sem("h1_hi_made"), sem("h2_hi_made")
        max_made, sub_made, sum_made, inv_made = sems("max_made", 2), sems("sub_made", 4), sems("sum_made", 2), sems("inv_made", 2)
        scaled1, scaled2, h1_lo_made, h2_lo_made = sem("scaled1"), sem("scaled2"), sem("h1_lo_made"), sem("h2_lo_made")
        stats1_made, stats2_made = sems("stats1_made", 2), sems("stats2_made", 2)
        mv1_made, mv2_made, xn1_made, xn2_made = sem("mv1_made"), sems("mv2_made", 2), sems("xn1_made", 2), sems("xn2_made", 2)
        g_hi_made, g_lo_made, att_lo_made = sems("g_hi_made", 4), sems("g_lo_made", 4), sems("att_lo_made", 4)
        o_biased, y_biased = sems("o_biased", 2), sems("y_biased", 2)
        var1_made, rstd1_made, var2_made, rstd2_made = sem("var1_made"), sem("rstd1_made"), sems("var2_made", 2), sems("rstd2_made", 2)
        norm_made, h1_made, h2_made = sems("norm_made", 4), sem("h1_made"), sem("h2_made")
        o_gated, x2_made, y_gated, y_made = sems("o_gated", 2), sems("x2_made", 2), sems("y_gated", 2), sems("y_made", 2)

        x_v = x.rearrange("b q d -> (b q) d").rearrange("(s t p) d -> s p t d", t=TILES, p=P)
        out_v = out.rearrange("b q d -> (b q) d").rearrange("(s t p) d -> s p t d", t=TILES, p=P)
        gates_v = gate_rows.rearrange("(s t b) g d -> s b g t d", t=TILES, b=2)


        PARTS = [(wqkv_hi[:, :, n:n + HALF], wqkv_lo[:, :, n:n + HALF], stage_q[:, :, n:n + HALF], stage_in[0], 16)
                 for n in range(0, INNER, HALF)]
        PARTS += [(wqkv_hi[:, :, n * INNER:(n + 1) * INNER], wqkv_lo[:, :, n * INNER:(n + 1) * INNER], stage, stage_in[n], 16)
                  for n, stage in ((1, stage_k), (2, stage_v))]
        Q_PARTS, K_PARTS, V_PARTS = 2, 3, 4
        by_rows = [(w, src, slice(i, i + 2), slice(0, DIM)) for w, src in (((wout_hi, wout_lo), w_out),) for i in range(0, PAIRS, 2)]
        by_rows += [((w1_hi, w1_lo), w1, slice(c, c + 1), slice(n, n + HALF)) for c in range(DC) for n in range(0, MLP, HALF)]
        by_rows += [((w2_hi, w2_lo), w2, slice(i, i + 2), slice(0, DIM)) for i in range(0, MC, 2)]
        small_sources = []
        for i, ((hi, lo), src, chunks, cols) in enumerate(by_rows):
            stage = small_stages[i % 3].rearrange("p (c n) -> p c n", c=chunks.stop - chunks.start)
            PARTS.append((hi[:, chunks, cols], lo[:, chunks, cols], stage, small_in[i % 3], 16 * (i // 3 + 1)))
            small_sources.append(src.rearrange("(c p) n -> p c n", p=P)[:, chunks, cols])
        SMALL = len(small_sources)
        OUT_PARTS, ALL_PARTS = V_PARTS + PAIRS // 2, len(PARTS)

        block = ctx.enter_context(nc.Block())

        @block.sync
        def _(sp):
            sp.dma_start(c_in, cond).then_inc(cond_in, 16)
            wmod_v = w_mod.rearrange("(c p) (g s n) -> p c g s n", p=P, g=2, s=3)
            sp.dma_start(wmod1, wmod_v[:, :, 0, 0:2, :].rearrange("p c s n -> p c (s n)")).then_inc(wmod1_in, 16)

            def load_x(d, turn):
                hold(sp, xn1_made[1], turn.before)
                src = x_v[d] if isinstance(d, int) else x_v[bass.ds(d, 1), :, :, :].squeeze(0)
                sp.dma_start(x_ln[:, :, :], src).then_inc(x_in, 16)

            def load_res(d, turn):
                hold(sp, x2_made[1], turn.before)
                src = x_v[d] if isinstance(d, int) else x_v[bass.ds(d, 1), :, :, :].squeeze(0)
                sp.dma_start(x_res[:, :, :], src).then_inc(xres_in, 16)
                load_gate(gate1, 0, d, gate1_in)

            def load_gate(tile, g, d, loaded):
                for b in range(2):
                    src = gates_v[d, b, g] if isinstance(d, int) else gates_v[bass.ds(d, 1), b, g, :, :].squeeze(0)
                    sp.dma_start(tile[SEQ * b:SEQ * (b + 1), :, :], src.partition_broadcast(SEQ)).then_inc(loaded, 16)

            def finish(d, turn):
                sp.wait_ge(y_made[0], turn.made)
                sp.wait_ge(y_made[1], turn.made)
                dst = out_v[d] if isinstance(d, int) else out_v[bass.ds(d, 1), :, :, :].squeeze(0)
                sp.dma_start(dst, y_buf[:, :, :]).then_inc(stored, 16)

            def load_small(i):
                if i >= 3:
                    sp.wait_ge(w_lo_made, V_PARTS + i - 2)
                sp.dma_start(PARTS[V_PARTS + i][2], small_sources[i]).then_inc(small_in[i % 3], 16)

            load_x(0, Turn(1, 0))
            sp.dma_start(bmod_col[:, :], b_mod.rearrange("(m p) -> p m", p=P),
                         allow_slow_non_contiguous=True).then_inc(bmod_in, 16)
            wqkv_v = w_qkv.rearrange("(c p) n -> p c n", p=P)
            sp.dma_start(stage_q, wqkv_v[:, :, 0:INNER]).then_inc(stage_in[0], 16)
            sp.dma_start(wmod2, wmod_v[:, :, 1, 0:2, :].rearrange("p c s n -> p c (s n)")).then_inc(wmod2_in, 16)
            sp.dma_start(stage_k, wqkv_v[:, :, INNER:2 * INNER]).then_inc(stage_in[1], 16)
            for g in range(2):
                sp.dma_start(wmod_g[:, :, g * DIM:(g + 1) * DIM], wmod_v[:, :, g, 2, :]).then_inc(gates_w_in, 16)
            sp.dma_start(gate_bias, b_mod.rearrange("(g s n) -> g s n", g=2, s=3)[:, 2, :].partition_broadcast(BATCH)).then_inc(gates_w_in, 16)
            sp.dma_start(stage_v, wqkv_v[:, :, 2 * INNER:]).then_inc(stage_in[2], 16)
            load_x(1, Turn(2, 1))
            sp.dma_start(bout_bc[:, :], b_out.partition_broadcast(P)).then_inc(consts_in, 16)
            sp.dma_start(b2_bc[:, :], b2.partition_broadcast(P)).then_inc(consts_in, 16)
            sp.dma_start(b1_col[:, :], b1.rearrange("(m p) -> p m", p=P),
                         allow_slow_non_contiguous=True).then_inc(consts_in, 16)
            for i in range(3):
                load_small(i)
            sp.wait_ge(gates_made, 1)
            sp.dma_start(gate_rows, gates).then_inc(stored, 16)
            for i in range(3, 6):
                load_small(i)
            sp.wait_ge(stored, 16)
            load_res(0, Turn(1, 0))
            load_gate(gate2, 1, 0, gate2_in)
            for i in range(6, SMALL):
                load_small(i)

            def step(s, has_next=True):
                prev, this, nxt = turns(sp, s)
                if has_next:
                    load_x(s + 1 if isinstance(s, int) else sp.snap(s + 1), nxt)
                load_res(s, this)
                finish(s - 1 if isinstance(s, int) else sp.snap(s - 1), prev)
                load_gate(gate2, 1, s, gate2_in)

            with sp.Fori(1, STEPS - 1) as s:
                step(s)
            step(STEPS - 1, has_next=False)
            for t in range(TILES):
                sp.wait_ge(y_made[t], STEPS)
                sp.dma_start(out_v[STEPS - 1][:, t, :], y_buf[:, t, :]).then_inc(stored, 16)
            sp.wait_ge(stored, 16 * (STEPS + TILES))

        @block.tensor
        def _(pe):
            drained = {}

            def three_products(ps, terms, done=None, first=True, final=True):
                n = len(terms)
                for i, (a_hi, a_lo, b_hi, b_lo) in enumerate(terms):
                    pe_mm(ps, a_hi, b_hi, first and i == 0, False)
                    pe_mm(ps, a_hi, b_lo, False, False)
                    last = pe_mm(ps, a_lo, b_hi, False, final and i == n - 1)
                if done is not None:
                    last.then_inc(done, 1)

            def pe_mm(ps, a, b, start, stop):
                return nc.tensor.matmul(ps, a, b, start=start, stop=stop)

            def scores(t, half, this):
                hold(pe, sub_made[2 * (1 - t) + half], this.before if t == 0 else this.made)
                if half == 0 and t == 0:
                    for u in range(8):
                        pe.wait_ge(qk_made[u], this.made)
                apart(pe, pe_passed, this.made)
                for i in range(HP):
                    pair = HP * half + i
                    for b in range(2):
                        tok = slice(t * P + b * SEQ, t * P + (b + 1) * SEQ)
                        for h in range(2):
                            rows = slice(DH * h, DH * (h + 1))
                            last = pe_mm(s_ps[half][rows, i * P + b * SEQ:i * P + (b + 1) * SEQ],
                                         qk[rows, pair, tok], qk[rows, PAIRS + pair, tok], True, True)
                last.then_inc(s_done[2 * t + half], 1)

            def values(u, this):
                t, n = divmod(u, 2)
                bank = BANK[f"v{u}"]
                hold(pe, *drained[bank])
                if u == 0:
                    pe.wait_ge(h1_hi_made, this.made)
                    pe.wait_ge(h1_lo_made, this.made)
                tok, cols = slice(t * P, (t + 1) * P), slice(2 * INNER + n * HALF, 2 * INNER + (n + 1) * HALF)
                three_products(dense[bank][:, :, :].rearrange("p a b -> p (a b)"),
                               [(h1_hi[:, c, tok], h1_lo[:, c, tok], wqkv_hi[:, c, cols], wqkv_lo[:, c, cols])
                                for c in range(DC)], v_done[u])
                drained[bank] = (v_made[u], this.made)

            def transposed(xn, bank, made, done, turn, tiles=range(TILES)):
                hold(pe, *drained[bank])
                for t in tiles:
                    pe.wait_ge(made[t], turn.made)
                for t in tiles:
                    for c in range(DC):
                        last = nc.tensor.transpose(dense[bank][:, c, t * P:(t + 1) * P], xn[:, t, c * P:(c + 1) * P], ident[:, :])
                last.then_inc(done, 1)

            def rows1_transposed(nxt):
                transposed(xn1, BANK["ln1t"], xn1_made, ln1t_done, nxt)
                drained[BANK["ln1t"]] = (scaled1, nxt.made)

            def rows2_transposed(prev):
                transposed(xn2, BANK["ln2t"], xn2_made, ln2t_done, prev)
                drained[BANK["ln2t"]] = (scaled2, prev.made)

            def ff1(u, prev, banks=BANK, h2_parts=0):
                bank = banks[f"ff1_{u}"]
                hold(pe, *drained[bank])
                if u == 0:
                    pe.wait_ge(h2_hi_made, h2_parts or prev.made)
                    pe.wait_ge(h2_lo_made, h2_parts or prev.made)
                for j in range(2):
                    cols = slice((2 * u + j) * P, (2 * u + j + 1) * P)
                    three_products(dense[bank][:, j, :],
                                   [(w1_hi[:, c, cols], w1_lo[:, c, cols], h2_hi[:, c, :], h2_lo[:, c, :])
                                    for c in range(DC)], ff1_done[u] if j == 1 else None)
                drained[bank] = (gelu_made[u], prev.made)

            def project_qk(u, nxt):
                bank = BANK[f"qk{u}"]
                hold(pe, *drained[bank])
                if u == 0:
                    pe.wait_ge(h1_hi_made, nxt.made)
                    pe.wait_ge(h1_lo_made, nxt.made)
                for j in range(2):
                    cols = slice((2 * u + j) * P, (2 * u + j + 1) * P)
                    three_products(dense[bank][:, j, :],
                                   [(wqkv_hi[:, c, cols], wqkv_lo[:, c, cols], h1_hi[:, c, :], h1_lo[:, c, :])
                                    for c in range(DC)], qk_done[u] if j == 1 else None)
                drained[bank] = (qk_made[u], nxt.made)

            def transpose_probs(t, half, this):
                n = 2 * t + half
                if n == 0:
                    hold(pe, pt_made[3], this.before)
                else:
                    pe.wait_ge(pt_made[n - 1], this.made)
                pe.wait_ge(norm_made[n], this.made)
                for i in range(HP):
                    last = nc.tensor.transpose(pt_ps[:, i * P:(i + 1) * P], probs[:, t, half, i * P:(i + 1) * P], ident[:, :])
                last.then_inc(pt_done[n], 1)

            def attend(t, half, this):
                if half == 0:
                    for u in (2 * t, 2 * t + 1):
                        pe.wait_ge(v_made[u], this.made)
                hold(pe, att_lo_made[2 * (1 - t) + half], this.before if t == 0 else this.made)
                pe.wait_ge(pt_made[2 * t + half], this.made)
                apart(pe, pe_passed, this.made)
                for i in range(HP):
                    for h in range(2):
                        head = 2 * (HP * half + i) + h
                        last = pe_mm(av_ps[half][DH * h:DH * (h + 1), i * P:(i + 1) * P],
                                     v[:, t, head * DH:(head + 1) * DH],
                                     probs_t[:, half, i, h, :, :].rearrange("p b q -> p (b q)"), True, True)
                last.then_inc(av_done[2 * t + half], 1)

            def project_out(t, this, banks=BANK, pairs=range(PAIRS)):
                bank, first, final = banks[f"o{t}"], pairs[0] == 0, pairs[-1] == PAIRS - 1
                if first:
                    hold(pe, *drained[bank])
                    for half in range(2):
                        pe.wait_ge(att_hi_made[2 * t + half], this.made)
                        pe.wait_ge(att_lo_made[2 * t + half], this.made)
                three_products(dense[bank][:, 0, :],
                               [(att_hi[:, t, c, :], att_lo[:, t, c, :], wout_hi[:, c, :], wout_lo[:, c, :])
                                for c in pairs], o_done[t] if final else None, first, final)
                drained[bank] = (o_biased[t], this.made)

            def ff2(t, prev, banks=BANK, units=range(4)):
                bank = banks[f"ff2_{t}"]
                if units[0] == 0:
                    hold(pe, *drained[bank])
                tok = slice(t * P, (t + 1) * P)
                for u in units:
                    if t == 0:
                        pe.wait_ge(g_hi_made[u], prev.made)
                        pe.wait_ge(g_lo_made[u], prev.made)
                    three_products(dense[bank][:, 0, :],
                                   [(g_hi[:, m, tok], g_lo[:, m, tok], w2_hi[:, m, :], w2_lo[:, m, :])
                                    for m in (2 * u, 2 * u + 1)], ff2_done[t] if u == 3 else None, u == 0, u == 3)
                drained[bank] = (y_biased[t], prev.made)

            def split(parts):
                pe.wait_ge(w_hi_made, parts)
                pe.wait_ge(w_lo_made, parts)

            def left_by_step(prev, this):
                drained[BANK["o1"]] = (o_biased[1], prev.made)
                drained[BANK["o0"]], drained[BANK["qk7"]] = (o_biased[0], prev.made), (qk_made[7], this.made)

            def first_step():
                _, this, nxt = turns(pe, 0)
                split(V_PARTS)
                values(0, this)
                scores(0, 0, this)
                values(1, this)
                scores(0, 1, this)
                values(2, this)
                values(3, this)
                rows1_transposed(nxt)
                scores(1, 0, this)
                pe.wait_ge(mod_made, 4)
                pe.wait_ge(gates_made, 1)
                transpose_probs(0, 0, this)
                scores(1, 1, this)
                transpose_probs(0, 1, this)
                pe.wait_ge(filled, 5)
                attend(0, 0, this)
                attend(0, 1, this)
                project_qk(0, nxt)
                project_qk(1, nxt)
                transpose_probs(1, 0, this)
                project_qk(2, nxt)
                transpose_probs(1, 1, this)
                project_qk(3, nxt)
                attend(1, 0, this)
                project_qk(4, nxt)
                split(OUT_PARTS)
                project_out(0, this)
                attend(1, 1, this)
                for u in range(5, 8):
                    project_qk(u, nxt)
                project_out(1, this)

            def step(s):
                prev, this, nxt = turns(pe, s)
                left_by_step(prev, this)
                scores(0, 0, this)
                scores(0, 1, this)
                values(0, this)
                values(1, this)
                rows2_transposed(prev)
                scores(1, 0, this)
                scores(1, 1, this)
                values(2, this)
                values(3, this)
                rows1_transposed(nxt)
                for u in range(4):
                    ff1(u, prev)
                for u in range(7):
                    project_qk(u, nxt)
                attend(0, 0, this)
                attend(0, 1, this)
                ff2(0, prev)
                ff2(1, prev)
                project_out(0, this, pairs=range(0, HP))
                attend(1, 0, this)
                attend(1, 1, this)
                project_out(0, this, pairs=range(HP, PAIRS))
                project_qk(7, nxt)
                project_out(1, this)

            def last_step():
                prev, this, _ = turns(pe, STEPS - 1)
                left_by_step(prev, this)
                scores(0, 0, this)
                scores(0, 1, this)
                values(0, this)
                values(1, this)
                rows2_transposed(prev)
                scores(1, 0, this)
                scores(1, 1, this)
                values(2, this)
                values(3, this)
                transpose_probs(0, 0, this)
                ff1(0, prev)
                transpose_probs(0, 1, this)
                attend(0, 0, this)
                ff1(1, prev)
                attend(0, 1, this)
                transpose_probs(1, 0, this)
                ff1(2, prev)
                ff1(3, prev)
                transpose_probs(1, 1, this)
                attend(1, 0, this)
                attend(1, 1, this)
                project_out(0, this, LAST_BANK)
                project_out(1, this, LAST_BANK)
                ff2(0, prev, LAST_BANK)
                transposed(xn2, END_BANK["ln2t"], xn2_made, ln2t_done, this, range(0, 1))
                drained[END_BANK["ln2t"]] = (scaled2, this.made)
                ff2(1, prev, LAST_BANK, range(0, 2))
                transposed(xn2, END_BANK["ln2t"], xn2_made, ln2t_done, this, range(1, 2))
                drained[END_BANK["ln2t"]] = (scaled2, this.made + 1)
                ff2(1, prev, LAST_BANK, range(2, 4))
                for u in range(4):
                    ff1(u, this, END_BANK, this.made + 1)
                for units in (range(0, 3), range(3, 4)):
                    for t in range(TILES):
                        ff2(t, this, END_BANK, units)

            pe.wait_ge(ident_made, 1)
            pe.wait_ge(cond_in, 16)
            for c in range(DC):
                last = nc.tensor.transpose(s_ps[0][:, c * BATCH:(c + 1) * BATCH], c_in[:, c * P:(c + 1) * P], ident[0:BATCH, 0:BATCH])
            last.then_inc(c_t_done, 1)

            def modulation(ps, w):
                for m in range(2 * DC):
                    for kc in range(DC):
                        last = pe_mm(ps[:, m * BATCH:(m + 1) * BATCH], w[:, kc, m * P:(m + 1) * P], silu_t[:, kc, :],
                                     kc == 0, kc == DC - 1)
                last.then_inc(mod_ps, 1)

            pe.wait_ge(silu_t_made, 1)
            pe.wait_ge(wmod1_in, 16)
            modulation(av_ps[0], wmod1)

            first = Turn(1, 0)
            drained.update({b: (mod_ps, 0) for b in range(3)})
            rows1_transposed(first)
            pe.wait_ge(wmod2_in, 16)
            modulation(pt_ps, wmod2)
            for u in range(4):
                if u % 2 == 0:
                    split(1 + u // 2)
                project_qk(u, first)
            pe.wait_ge(gates_w_in, 48)
            for kc in range(DC):
                last = pe_mm(av_ps[1][0:BATCH, :], silu_t[:, kc, :], wmod_g[:, kc, :], kc == 0, kc == DC - 1)
            last.then_inc(mod_ps, 1)
            split(K_PARTS)
            for u in range(4, 8):
                project_qk(u, first)
            first_step()
            split(ALL_PARTS)
            with pe.Fori(1, STEPS - 1) as s:
                step(s)
            last_step()

        @block.scalar
        def _(act):
            def copy_bank(dst, src, made):
                nc.scalar.activation(dst, src, ACT.Copy).then_inc(made, 1)

            def high_part(dst, src, whole_made, made, count, cols=slice(0, TOK)):
                act.wait_ge(whole_made, count)
                nc.scalar.activation(dst[:, :, cols], src[:, :, cols], ACT.Copy).then_inc(made, 1)

            def flat(ps):
                return ps[:, :, :].rearrange("p a b -> p (a b)")

            def exp(t, half, this):
                n = 2 * t + half
                act.wait_ge(sub_made[n], this.made)
                e = probs[:, t, half, :]
                nc.scalar.activation(e, e, ACT.Exp, scale=DH ** -0.5).then_inc(exp_made[n], 1)

            def take_v(u, this):
                act.wait_ge(v_done[u], this.made)
                t, n = divmod(u, 2)
                copy_bank(v[:, t, n * HALF:(n + 1) * HALF], flat(dense[BANK[f"v{u}"]]), v_made[u])

            def take_qk(u, nxt):
                act.wait_ge(qk_done[u], nxt.made)
                bank = BANK[f"qk{u}"]
                copy_bank(qk[:, 2 * u:2 * u + 2, :], dense[bank][:, :, :], qk_made[u])

            def gelus(u, prev, banks=BANK):
                act.wait_ge(ff1_done[u], prev.made)
                if u >= 2:
                    act.wait_ge(g_lo_made[u - 2], prev.made)
                for j in range(2):
                    m = 2 * u + j
                    last = nc.scalar.activation(gelu[:, u % 2, j * TOK:(j + 1) * TOK], dense[banks[f"ff1_{u}"]][:, j, :], ACT.Gelu,
                                                bias=b1_col[:, m:m + 1])
                last.then_inc(gelu_made[u], 1)

            def take_pt(t, half, this):
                n = 2 * t + half
                act.wait_ge(pt_done[n], 1 if this.before == 0 else 2)
                for b in range(2):
                    rows = slice(SEQ * b, SEQ * (b + 1))
                    last = nc.scalar.activation(probs_t[rows, half, :, :, b, :],
                                                pt_ps[rows, :].rearrange("p (i h q) -> p i h q", i=HP, h=2), ACT.Copy)
                last.then_inc(pt_made[n], 1)

            def att_high(t, half, this):
                n = 2 * t + half
                act.wait_ge(av_done[n], this.made)
                copy_bank(att_hi[:, t, HP * half:HP * (half + 1), :], av_ps[half][:, :].rearrange("p (i q) -> p i q", i=HP),
                          att_hi_made[n])

            def scores_and_values(this, prev):
                exp(0, 0, this)
                take_v(0, this)
                take_v(1, this)
                exp(0, 1, this)
                high_part(h2_hi, h2, h2_made, h2_hi_made, prev.made)
                exp(1, 0, this)
                take_v(2, this)

            def first_step():
                _, this, nxt = turns(act, 0)
                take_v(0, this)
                exp(0, 0, this)
                split_high(V_PARTS + 3)
                take_v(1, this)
                exp(0, 1, this)
                take_v(2, this)
                split_high(V_PARTS + 4)
                take_v(3, this)
                split_high(V_PARTS + 5)
                act.wait_ge(w_lo_made, V_PARTS)
                take_pt(0, 0, this)
                exp(1, 0, this)
                take_pt(0, 1, this)
                high_part(h1_hi, h1, h1_made, h1_hi_made, nxt.made)
                exp(1, 1, this)
                split_high(V_PARTS + 6)
                att_high(0, 0, this)
                split_high(V_PARTS + 7)
                att_high(0, 1, this)
                split_high(V_PARTS + 8)
                take_qk(0, nxt)
                take_qk(1, nxt)
                take_pt(1, 0, this)
                take_qk(2, nxt)
                take_pt(1, 1, this)
                take_qk(3, nxt)
                split_high(V_PARTS + 9)
                att_high(1, 0, this)
                take_qk(4, nxt)
                split_high(V_PARTS + 10)
                att_high(1, 1, this)
                split_high(V_PARTS + 11)
                for u in range(5, 8):
                    take_qk(u, nxt)

            def step(s):
                prev, this, nxt = turns(act, s)
                scores_and_values(this, prev)
                take_v(3, this)
                exp(1, 1, this)
                gelus(0, prev)
                high_part(h1_hi, h1, h1_made, h1_hi_made, nxt.made)
                for u in range(1, 4):
                    gelus(u, prev)
                for u in range(7):
                    take_qk(u, nxt)
                att_high(0, 0, this)
                att_high(0, 1, this)
                att_high(1, 0, this)
                att_high(1, 1, this)
                take_qk(7, nxt)

            def last_step():
                prev, this, _ = turns(act, STEPS - 1)
                scores_and_values(this, prev)
                take_v(3, this)
                take_pt(0, 0, this)
                exp(1, 1, this)
                take_pt(0, 1, this)
                gelus(0, prev)
                gelus(1, prev)
                att_high(0, 0, this)
                att_high(0, 1, this)
                take_pt(1, 0, this)
                gelus(2, prev)
                take_pt(1, 1, this)
                gelus(3, prev)
                att_high(1, 0, this)
                att_high(1, 1, this)
                for t in range(TILES):
                    high_part(h2_hi, h2, h2_made, h2_hi_made, this.made + t, slice(t * P, (t + 1) * P))
                for u in range(4):
                    gelus(u, this, END_BANK)

            act.wait_ge(c_t_done, 1)
            nc.scalar.activation(c_exp, s_ps[0][:, 0:DC * BATCH], ACT.Exp, scale=-1.0).then_inc(c_exp_made, 1)
            first = Turn(1, 0)

            def split_high(i):
                hi, _, src, arrived, count = PARTS[i]
                act.wait_ge(arrived, count)
                nc.scalar.activation(hi, src, ACT.Copy).then_inc(w_hi_made, 1)

            for i in range(Q_PARTS):
                split_high(i)
            high_part(h1_hi, h1, h1_made, h1_hi_made, 1)
            split_high(Q_PARTS)
            take_qk(0, first)
            take_qk(1, first)
            split_high(K_PARTS)
            take_qk(2, first)
            take_qk(3, first)
            for i in range(3):
                take_qk(4 + i, first)
                split_high(V_PARTS + i)
            take_qk(7, first)
            act.wait_ge(consts_in, 48)
            first_step()
            act.wait_ge(w_lo_made, ALL_PARTS)
            with act.Fori(1, STEPS - 1) as s:
                step(s)
            last_step()

        @block.vector
        def _(dve):
            def heads(ap):
                return ap.rearrange("p (g k) -> p g k", k=SEQ)

            def by_row(ap):
                return ap.unsqueeze(2).to_broadcast([P, 2 * HP, SEQ])

            def maxima(t, half, this):
                n = 2 * t + half
                dve.wait_ge(s_done[n], this.made)
                nc.vector.tensor_reduce(row_max[:, t, half, :], heads(s_ps[half][:, :]), AX.X, ALU.max).then_inc(max_made[t], 1)

            def subtract(t, half, this):
                n = 2 * t + half
                dve.wait_ge(max_made[t], this.halves[half])
                nc.vector.tensor_tensor(heads(probs[:, t, half, :]), heads(s_ps[half][:, :]), by_row(row_max[:, t, half, :]),
                                        ALU.subtract).then_inc(sub_made[n], 1)

            def sums(t, half, this):
                n = 2 * t + half
                dve.wait_ge(exp_made[n], this.made)
                nc.vector.tensor_reduce(row_sum[:, t, half, :], heads(probs[:, t, half, :]), AX.X, ALU.add).then_inc(sum_made[t], 1)
                dve.wait_ge(sum_made[t], this.halves[half])
                nc.vector.reciprocal(row_inv[:, t, half, :], row_sum[:, t, half, :]).then_inc(inv_made[t], 1)

            def row_stats(src, t, stats, mv, stats_made, mv_done, turn):
                nc.vector.bn_stats(stats[:, t, :], src[:, t, :]).then_inc(stats_made[t], 1)
                dve.wait_ge(stats_made[t], turn.made)
                apart(dve, dve_passed, turn.made)
                last = nc.vector.bn_aggr(mv[:, t, :], stats[:, t, :])
                if mv_done is not None:
                    last.then_inc(mv_done, 1)

            def normalise(src, t, mv, rstd, dst, made):
                nc.vector.tensor_scalar(dst[:, t, :], src[:, t, :], mv[:, t, 0:1], rstd[:, t:t + 1],
                                        ALU.subtract, ALU.mult).then_inc(made[t], 1)

            def ln1_stats(turn, loaded):
                dve.wait_ge(x_in, loaded)
                for t in range(TILES):
                    row_stats(x_ln, t, stats1, mv1, stats1_made, mv1_made if t == 1 else None, turn)

            def ln1_rows(turn):
                dve.wait_ge(rstd1_made, turn.made)
                for t in range(TILES):
                    normalise(x_ln, t, mv1, rstd1, xn1, xn1_made)

            def scale(bank, section, h, done, made, d, count, tiles=range(TILES)):
                dve.wait_ge(done, count)
                n, cols = 2 * len(tiles), slice(tiles[0] * P, (tiles[-1] + 1) * P)
                at_b = slice(d * NB + 2 * tiles[0], d * NB + 2 * tiles[0] + n) if isinstance(d, int) else bass.ds(d * NB, NB)
                nc.vector.tensor_tensor(h[:, :, cols].rearrange("p c (b k) -> p c b k", b=n),
                                        dense[bank][:, :, cols].rearrange("p c (b k) -> p c b k", b=n),
                                        mod_t[:, section, :, at_b].unsqueeze(3).to_broadcast([P, DC, n, SEQ]),
                                        ALU.mult).then_inc(made, 1)

            def scale1(d, nxt):
                scale(BANK["ln1t"], SC1, h1, ln1t_done, scaled1, d, nxt.made)

            def scale2(d, prev):
                scale(BANK["ln2t"], SC2, h2, ln2t_done, scaled2, d, prev.made)

            def scale_last(t, this):
                scale(END_BANK["ln2t"], SC2, h2, ln2t_done, scaled2, STEPS - 1, this.made + t, range(t, t + 1))

            def low_part(lo, src, hi, hi_made, made, count, cols=slice(0, TOK)):
                dve.wait_ge(hi_made, count)
                nc.vector.tensor_tensor(lo[:, :, cols], src[:, :, cols], hi[:, :, cols].bitcast(F32), ALU.subtract).then_inc(made, 1)

            def h1_low(nxt):
                low_part(h1_lo, h1, h1_hi, h1_hi_made, h1_lo_made, nxt.made)

            def h2_low(prev):
                low_part(h2_lo, h2, h2_hi, h2_hi_made, h2_lo_made, prev.made)

            def gelu_parts(u):
                return gelu[:, u % 2, :].rearrange("p (a b) -> p a b", a=2), g_hi[:, 2 * u:2 * u + 2, :], g_lo[:, 2 * u:2 * u + 2, :]

            def gelu_high(u, prev):
                dve.wait_ge(gelu_made[u], prev.made)
                g, hi, _ = gelu_parts(u)
                nc.vector.tensor_copy(hi, g).then_inc(g_hi_made[u], 1)

            def gelu_low(u, prev):
                dve.wait_ge(g_hi_made[u], prev.made)
                g, hi, lo = gelu_parts(u)
                nc.vector.tensor_tensor(lo, g, hi.bitcast(F32), ALU.subtract).then_inc(g_lo_made[u], 1)

            def split_gelu(u, prev):
                gelu_high(u, prev)
                gelu_low(u, prev)

            def transpose_probs(t, half, parts, this):
                if parts[0] == 0:
                    dve.wait_ge(norm_made[2 * t + half], this.made)
                    dve.wait_ge(av_done[2 * (1 - t) + half], this.before if t == 0 else this.made)
                    apart(dve, dve_passed, this.made)
                src = probs[:, t, half, :].rearrange("p (i n) -> p i n", i=HP)
                for part in parts:
                    h, q = divmod(part * BLOCK, SEQ)
                    for c in range(0, P, BLOCK):
                        last = nc.vector.transpose(probs_t[c:c + BLOCK, half, :, h, c // SEQ, q:q + BLOCK],
                                                   src[part * BLOCK:(part + 1) * BLOCK, :, c:c + BLOCK])
                if parts[-1] == P // BLOCK - 1:
                    last.then_inc(pt_made[2 * t + half], 1)

            def att_low(t, half, this):
                n = 2 * t + half
                dve.wait_ge(att_hi_made[n], this.made)
                pairs = slice(HP * half, HP * (half + 1))
                nc.vector.tensor_tensor(att_lo[:, t, pairs, :], av_ps[half][:, :].rearrange("p (i q) -> p i q", i=HP),
                                        att_hi[:, t, pairs, :].bitcast(F32), ALU.subtract).then_inc(att_lo_made[n], 1)

            def add_bias(t, bank, done, bias, dst, made, turn):
                dve.wait_ge(done[t], turn.made)
                nc.vector.tensor_tensor(dst[:, t, :], dense[bank][:, 0, :], bias[:, :], ALU.add).then_inc(made[t], 1)

            def ln2_stats(t, this, rows=x2):
                dve.wait_ge(x2_made[t], this.made)
                row_stats(rows, t, stats2, mv2, stats2_made, mv2_made[t], this)

            def ln2_rows(t, this, rows=x2):
                dve.wait_ge(rstd2_made[t], this.made)
                normalise(rows, t, mv2, rstd2, xn2, xn2_made)

            def project_biased(t, this, banks=BANK):
                add_bias(t, banks[f"o{t}"], o_done, bout_bc, o_buf, o_biased, this)

            def mlp_biased(t, prev, stores, banks=BANK):
                if t == 0:
                    dve.wait_ge(stored, stores)
                add_bias(t, banks[f"ff2_{t}"], ff2_done, b2_bc, y_buf, y_biased, prev)

            def gated_sum(t, buf, biased, gate, gated, addend, dst, made, turn):
                dve.wait_ge(biased[t], turn.made)
                nc.vector.tensor_tensor(buf[:, t, :], buf[:, t, :], gate[:, t, :], ALU.mult).then_inc(gated[t], 1)
                dve.wait_ge(gated[t], turn.made)
                nc.vector.tensor_tensor(dst[:, t, :], buf[:, t, :], addend[:, t, :], ALU.add).then_inc(made[t], 1)

            def split_low(i):
                dve.wait_ge(w_hi_made, i + 1)
                hi, lo, src, _, _ = PARTS[i]
                nc.vector.tensor_tensor(lo, src, hi.bitcast(F32), ALU.subtract).then_inc(w_lo_made, 1)

            def first_step():
                _, this, nxt = turns(dve, 0)
                count_halves(dve, 0, this)
                maxima(0, 0, this)
                subtract(0, 0, this)
                maxima(0, 1, this)
                subtract(0, 1, this)
                split_low(V_PARTS + 3)
                sums(0, 0, this)
                sums(0, 1, this)
                scale1(1, nxt)
                maxima(1, 0, this)
                subtract(1, 0, this)
                split_low(V_PARTS + 4)
                maxima(1, 1, this)
                subtract(1, 1, this)
                split_low(V_PARTS + 5)
                h1_low(nxt)
                sums(1, 0, this)
                sums(1, 1, this)
                split_low(V_PARTS + 6)
                att_low(0, 0, this)
                split_low(V_PARTS + 7)
                att_low(0, 1, this)
                for i in range(8, 10):
                    split_low(V_PARTS + i)
                att_low(1, 0, this)
                split_low(V_PARTS + 10)
                project_biased(0, this)
                att_low(1, 1, this)
                split_low(V_PARTS + 11)
                ln2_stats(0, this)
                ln2_rows(0, this)
                project_biased(1, this)

            def step(s):
                prev, this, nxt = turns(dve, s)
                count_halves(dve, s, this)
                stores, loads = dve.snap(s * 16), dve.snap(s * 16 + 32)
                maxima(0, 0, this)
                ln2_stats(1, prev)
                subtract(0, 0, this)
                ln2_rows(1, prev)
                maxima(0, 1, this)
                subtract(0, 1, this)
                sums(0, 0, this)
                scale2(dve.snap(s - 1), prev)
                ln1_stats(nxt, loads)
                maxima(1, 0, this)
                subtract(1, 0, this)
                ln1_rows(nxt)
                h2_low(prev)
                maxima(1, 1, this)
                subtract(1, 1, this)
                scale1(dve.snap(s + 1), nxt)
                sums(0, 1, this)
                sums(1, 0, this)
                gelu_high(0, prev)
                h1_low(nxt)
                gelu_low(0, prev)
                split_gelu(1, prev)
                transpose_probs(0, 0, range(0, 4), this)
                split_gelu(2, prev)
                split_gelu(3, prev)
                transpose_probs(0, 1, range(0, 4), this)
                sums(1, 1, this)
                transpose_probs(1, 0, range(0, 1), this)
                att_low(0, 0, this)
                transpose_probs(1, 0, range(1, 2), this)
                att_low(0, 1, this)
                transpose_probs(1, 0, range(2, 4), this)
                mlp_biased(0, prev, stores)
                transpose_probs(1, 1, range(0, 4), this)
                mlp_biased(1, prev, stores)
                att_low(1, 0, this)
                att_low(1, 1, this)
                project_biased(0, this)
                ln2_stats(0, this)
                ln2_rows(0, this)
                project_biased(1, this)

            def last_step():
                prev, this, _ = turns(dve, STEPS - 1)
                count_halves(dve, STEPS - 1, this)
                maxima(0, 0, this)
                ln2_stats(1, prev)
                subtract(0, 0, this)
                ln2_rows(1, prev)
                maxima(0, 1, this)
                subtract(0, 1, this)
                sums(0, 0, this)
                scale2(STEPS - 2, prev)
                sums(0, 1, this)
                maxima(1, 0, this)
                subtract(1, 0, this)
                h2_low(prev)
                maxima(1, 1, this)
                subtract(1, 1, this)
                sums(1, 0, this)
                sums(1, 1, this)
                split_gelu(0, prev)
                split_gelu(1, prev)
                att_low(0, 0, this)
                att_low(0, 1, this)
                split_gelu(2, prev)
                split_gelu(3, prev)
                att_low(1, 0, this)
                att_low(1, 1, this)
                project_biased(0, this, LAST_BANK)
                ln2_stats(0, this, x2_last)
                project_biased(1, this, LAST_BANK)
                dve.wait_ge(gate1_in, 32 * STEPS)
                dve.wait_ge(xres_in, 16 * STEPS)
                gated_sum(1, o_buf, o_biased, gate1, o_gated, x_res, x2_last, x2_made, this)
                ln2_rows(0, this, x2_last)
                ln2_stats(1, this, x2_last)
                mlp_biased(0, prev, 16 * (STEPS - 1), LAST_BANK)
                scale_last(0, this)
                ln2_rows(1, this, x2_last)
                scale_last(1, this)
                for t in range(TILES):
                    low_part(h2_lo, h2, h2_hi, h2_hi_made, h2_lo_made, this.made + t, slice(t * P, (t + 1) * P))
                mlp_biased(1, prev, 16 * (STEPS - 1), LAST_BANK)
                for u in range(4):
                    split_gelu(u, this)
                mlp_biased(0, this, 16 * STEPS, END_BANK)
                mlp_biased(1, this, 16 * STEPS, END_BANK)
                dve.wait_ge(gate2_in, 32 * STEPS)
                gated_sum(1, y_buf, y_biased, gate2, y_gated, x2_last, y_buf, y_made, this)

            dve.wait_ge(c_exp_made, 1)
            nc.vector.tensor_scalar(c_exp, c_exp, 1.0, None, ALU.add).then_inc(silu_step, 1)
            dve.wait_ge(silu_step, 1)
            nc.vector.reciprocal(c_exp, c_exp).then_inc(silu_step, 1)
            dve.wait_ge(silu_step, 2)
            nc.vector.tensor_tensor(silu_flat, s_ps[0][:, 0:DC * BATCH], c_exp, ALU.mult).then_inc(silu_t_made, 1)
            first, second = Turn(1, 0), Turn(2, 1)
            ln1_stats(first, 16)
            ln1_rows(first)

            def modulation(section, col, ps):
                nc.vector.tensor_tensor(mod_t[:, section, :, :], ps.rearrange("p (c b) -> p c b", c=DC),
                                        bmod_col[:, col:col + DC].unsqueeze(2).to_broadcast([P, DC, BATCH]), ALU.add).then_inc(mod_made, 1)

            dve.wait_ge(bmod_in, 16)
            scale_bias = bmod_col[:, :].rearrange("p (g m) -> p g m", g=2)[:, :, DC:2 * DC]
            nc.vector.tensor_scalar(scale_bias, scale_bias, 1.0, None, ALU.add).then_inc(bias_made, 1)
            dve.wait_ge(bias_made, 1)
            dve.wait_ge(mod_ps, 1)
            modulation(SC1, DC, av_ps[0][:, DC * BATCH:2 * DC * BATCH])
            modulation(SH1, 0, av_ps[0][:, 0:DC * BATCH])
            dve.wait_ge(mod_made, 2)
            scale1(0, first)
            split_low(0)
            h1_low(first)
            split_low(1)
            split_low(2)
            split_low(3)
            dve.wait_ge(mod_ps, 2)
            modulation(SH2, 3 * DC, pt_ps[:, 0:DC * BATCH])
            modulation(SC2, 4 * DC, pt_ps[:, DC * BATCH:2 * DC * BATCH])
            dve.wait_ge(mod_ps, 3)
            nc.vector.tensor_tensor(gates, av_ps[1][0:BATCH, :].rearrange("p (g d) -> p g d", g=2), gate_bias,
                                    ALU.add).then_inc(gates_made, 1)
            dve.wait_ge(mod_made, 4)
            ln1_stats(second, 32)
            for i in range(3):
                split_low(V_PARTS + i)
                if i == 0:
                    ln1_rows(second)
            dve.wait_ge(consts_in, 48)
            first_step()
            with dve.Fori(1, STEPS - 1) as s:
                step(s)
            last_step()

        @block.gpsimd
        def _(pool):
            def reciprocal_root(mv, var, rstd, var_done, rstd_done, count, width):
                nc.gpsimd.tensor_tensor(var, mv, eps[:, 0:width], ALU.add).then_inc(var_done, 1)
                pool.wait_ge(var_done, count)
                nc.gpsimd.tensor_tensor(rstd, var, minus_half[:, 0:width], ALU.pow).then_inc(rstd_done, 1)

            def ln1_root(turn):
                pool.wait_ge(mv1_made, turn.made)
                reciprocal_root(mv1[:, :, 1], var1[:, :], rstd1[:, :], var1_made, rstd1_made, turn.made, TILES)

            def ln2_root(t, turn):
                pool.wait_ge(mv2_made[t], turn.made)
                reciprocal_root(mv2[:, t, 1:2], var2[:, t:t + 1], rstd2[:, t:t + 1], var2_made[t], rstd2_made[t], turn.made, 1)

            def normalise_probs(t, half, this):
                pool.wait_ge(inv_made[t], this.halves[half])
                e = probs[:, t, half, :].rearrange("p (g k) -> p g k", k=SEQ)
                nc.gpsimd.tensor_tensor(e, e, row_inv[:, t, half, :].unsqueeze(2).to_broadcast([P, 2 * HP, SEQ]),
                                        ALU.mult).then_inc(norm_made[2 * t + half], 1)

            def shift(section, h, scaled, made, d, count, tiles=range(TILES)):
                pool.wait_ge(scaled, count)
                n, cols = 2 * len(tiles), slice(tiles[0] * P, (tiles[-1] + 1) * P)
                at_b = slice(d * NB + 2 * tiles[0], d * NB + 2 * tiles[0] + n) if isinstance(d, int) else bass.ds(d * NB, NB)
                hv = h[:, :, cols].rearrange("p c (b k) -> p c b k", b=n)
                nc.gpsimd.tensor_tensor(hv, hv, mod_t[:, section, :, at_b].unsqueeze(3).to_broadcast([P, DC, n, SEQ]),
                                        ALU.add).then_inc(made, 1)

            def gated_sum(t, buf, biased, gate, gated, addend, dst, made, turn):
                pool.wait_ge(biased[t], turn.made)
                nc.gpsimd.tensor_tensor(buf[:, t, :], buf[:, t, :], gate[:, t, :], ALU.mult).then_inc(gated[t], 1)
                pool.wait_ge(gated[t], turn.made)
                nc.gpsimd.tensor_tensor(dst[:, t, :], buf[:, t, :], addend[:, t, :], ALU.add).then_inc(made[t], 1)

            def mlp_sum(t, turn, rows=x2):
                gated_sum(t, y_buf, y_biased, gate2, y_gated, rows, y_buf, y_made, turn)

            def attention_sum(t, turn, rows=x2):
                gated_sum(t, o_buf, o_biased, gate1, o_gated, x_res, rows, x2_made, turn)

            def shift1(d, nxt):
                shift(SH1, h1, scaled1, h1_made, d, nxt.made)

            def shift2(d, prev):
                shift(SH2, h2, scaled2, h2_made, d, prev.made)

            def first_step():
                _, this, nxt = turns(pool, 0)
                count_halves(pool, 0, this)
                normalise_probs(0, 0, this)
                normalise_probs(0, 1, this)
                shift1(1, nxt)
                normalise_probs(1, 0, this)
                normalise_probs(1, 1, this)
                pool.wait_ge(gate1_in, 32)
                pool.wait_ge(xres_in, 16)
                attention_sum(0, this)
                ln2_root(0, this)
                attention_sum(1, this)

            def step(s):
                prev, this, nxt = turns(pool, s)
                count_halves(pool, s, this)
                ln2_root(1, prev)
                normalise_probs(0, 0, this)
                shift2(pool.snap(s - 1), prev)
                ln1_root(nxt)
                shift1(pool.snap(s + 1), nxt)
                normalise_probs(0, 1, this)
                normalise_probs(1, 0, this)
                normalise_probs(1, 1, this)
                pool.wait_ge(gate2_in, pool.snap(s * 32))
                mlp_sum(0, prev)
                mlp_sum(1, prev)
                pool.wait_ge(gate1_in, pool.snap(s * 32 + 32))
                pool.wait_ge(xres_in, pool.snap(s * 16 + 16))
                attention_sum(0, this)
                ln2_root(0, this)
                attention_sum(1, this)

            def last_step():
                prev, this, _ = turns(pool, STEPS - 1)
                count_halves(pool, STEPS - 1, this)
                ln2_root(1, prev)
                normalise_probs(0, 0, this)
                shift2(STEPS - 2, prev)
                normalise_probs(0, 1, this)
                normalise_probs(1, 0, this)
                normalise_probs(1, 1, this)
                pool.wait_ge(gate1_in, 32 * STEPS)
                pool.wait_ge(xres_in, 16 * STEPS)
                attention_sum(0, this, x2_last)
                for t in range(TILES):
                    ln2_root(t, this)
                for t in range(TILES):
                    shift(SH2, h2, scaled2, h2_made, STEPS - 1, this.made + t, range(t, t + 1))
                pool.wait_ge(gate2_in, 32 * (STEPS - 1))
                for t in range(TILES):
                    mlp_sum(t, prev)
                pool.wait_ge(gate2_in, 32 * STEPS)
                mlp_sum(0, this, x2_last)

            nc.gpsimd.memset(ident[:, :], 0.0).then_inc(filled, 1)
            nc.gpsimd.memset(minus_half[:, :], -0.5).then_inc(filled, 1)
            nc.gpsimd.memset(eps[:, :], EPS).then_inc(filled, 1)
            pool.wait_ge(filled, 3)
            nc.gpsimd.affine_select(out=ident[:, :], in_=ident[:, :], compare_op=ALU.not_equal, fill=1.0,
                                    base=0, pattern=[[-1, P]], channel_multiplier=1).then_inc(ident_made, 1)
            first = Turn(1, 0)
            ln1_root(first)
            pool.wait_ge(mod_made, 2)
            shift1(0, first)
            ln1_root(Turn(2, 1))
            pool.wait_ge(rstd1_made, 2)
            pool.wait_ge(w_lo_made, V_PARTS)
            for b in range(2):
                nc.gpsimd.memset(probs_t[SEQ * b:SEQ * (b + 1), :, :, :, 1 - b, :], 0.0).then_inc(filled, 1)
            pool.wait_ge(filled, 5)
            pool.wait_ge(mod_made, 4)
            first_step()
            with pool.Fori(1, STEPS - 1) as s:
                step(s)
            last_step()


_INS = ['x', 'cond_1024', 'L0_cond_W_mod', 'L0_cond_b_mod', 'L0_cond_W_qkv', 'L0_cond_W_out', 'L0_cond_b_out',
        'L0_cond_W1', 'L0_cond_b1', 'L0_cond_W2', 'L0_cond_b2']


def kernel(**inputs):
    import numpy as _np
    import concourse.bacc as _bacc
    from concourse import mybir as _mybir
    from concourse.bass_utils import run_bass_kernel_spmd as _run

    nc = _bacc.Bacc("TRN2", target_bir_lowering=False, num_devices=1)
    arrays, args = {}, []
    for name in _INS:
        a = _np.ascontiguousarray(inputs[name])
        arrays[f"in_{name}_dram"] = a
        args.append(nc.dram_tensor(f"in_{name}_dram", a.shape, _mybir.dt.from_np(a.dtype), kind="ExternalInput").ap())
    args.append(nc.dram_tensor("out_0_dram", (BATCH, SEQ, DIM), _mybir.dt.float32, kind="ExternalOutput").ap())
    dit_block_kernel(nc, *args)
    r = _run(nc, [arrays], core_ids=[0])
    return r.results[0]["out_0_dram"]
```
